# Optimizing a Trainium2 kernel written in Bass

```python
import numpy as np
import jax
import jax.numpy as jnp

def _softmax(x, axis=-1):
    return jax.nn.softmax(x, axis=axis)

def _gelu(x):
    return jax.nn.gelu(x, approximate=True)

def _silu(x):
    return jax.nn.silu(x)

def _sigmoid(x):
    return jax.nn.sigmoid(x)

def _layernorm(x, axis=-1, eps=1e-05):
    m = jnp.mean(x, axis=axis, keepdims=True)
    v = jnp.var(x, axis=axis, keepdims=True)
    return (x - m) / jnp.sqrt(v + eps)

def _scatter_add(tgt, idx, src, axis=0):
    return tgt.at[idx].add(src)

def _segment_sum(src, seg, n):
    return jax.ops.segment_sum(src, seg, n)
kernel_name = 'mk_adaln_ffn_d1_seqx_r4_50c2d7'

def setup_inputs(seed: int=0):
    np.random.seed(seed)
    _w = jnp.asarray

    def _rec_inputs():
        import jax
        import jax.numpy as jnp
        _rk = jax.random.key(seed)
        x = -1.394e-06 + 0.9999 * jax.random.normal(jax.random.fold_in(_rk, 1), (16, 256, 512), jnp.float32)
        _lenS = 256 - jax.random.randint(jax.random.fold_in(_rk, 7), (16,), 0, max(1, 256 // 4) + 1, jnp.int32)
        _lenS2 = 256 - jax.random.randint(jax.random.fold_in(_rk, 8), (16,), 0, max(1, 256 // 4) + 1, jnp.int32)
        cond_2048 = -0.00499425 + 1.0058 * jax.random.normal(jax.random.fold_in(_rk, 11), (16, 512), jnp.float32)
        return (x, cond_2048)
    x, cond_2048 = _rec_inputs()

    def _L0_cond_setup():
        import jax, jax.numpy as jnp
        import numpy as np
        B, T, D = (16, 128, 512)
        key = jax.random.key(seed)
        k0, k1, k2, k3 = jax.random.split(key, 4)
        scale = 1.0 / np.sqrt(D)
        return {'initial_state': jax.random.normal(k0, (B, D), jnp.float32), 'inputs': jax.random.normal(k1, (B, T, D), jnp.float32), 'W_ih': jax.random.normal(k2, (D, 3 * D), jnp.float32) * scale, 'W_hh': jax.random.normal(k3, (D, 3 * D), jnp.float32) * scale, 'b_ih': jnp.zeros((3 * D,), jnp.float32), 'b_hh': jnp.zeros((3 * D,), jnp.float32)}
    _L0_cond_all = _L0_cond_setup()
    _L0_cond_in = {k: v for k, v in _L0_cond_all.items() if k in ('W_ih', 'W_hh', 'b_ih', 'b_hh')}
    del _L0_cond_all

    def _L0_ffn_setup():
        import jax, jax.numpy as jnp
        import numpy as np
        NUM_EXPERTS = 16
        C = 1.0
        key = jax.random.key(seed)
        k1, k2, k3 = jax.random.split(key, 3)
        b, s, h = (4, 512, 512)
        return {'x': jax.random.normal(k1, (b, s, h), dtype=jnp.float32), 'router_w': jax.random.normal(k2, (h, NUM_EXPERTS), dtype=jnp.float32) * 0.02, 'router_b': jnp.zeros((NUM_EXPERTS,), dtype=jnp.float32), 'expert_w': jax.random.normal(k3, (h, h), dtype=jnp.float32) * 0.02, 'expert_b': jnp.zeros((h,), dtype=jnp.float32)}
    _L0_ffn_all = _L0_ffn_setup()
    _L0_ffn_in = {k: v for k, v in _L0_ffn_all.items() if k in ('router_w', 'router_b', 'expert_w', 'expert_b')}
    del _L0_ffn_all
    return {'x': x, 'cond_2048': cond_2048, 'L0_cond_W_ih': _L0_cond_in['W_ih'], 'L0_cond_W_hh': _L0_cond_in['W_hh'], 'L0_cond_b_ih': _L0_cond_in['b_ih'], 'L0_cond_b_hh': _L0_cond_in['b_hh'], 'L0_ffn_router_w': _L0_ffn_in['router_w'], 'L0_ffn_router_b': _L0_ffn_in['router_b'], 'L0_ffn_expert_w': _L0_ffn_in['expert_w'], 'L0_ffn_expert_b': _L0_ffn_in['expert_b']}

def reference(x, cond_2048, L0_cond_W_ih, L0_cond_W_hh, L0_cond_b_ih, L0_cond_b_hh, L0_ffn_router_w, L0_ffn_router_b, L0_ffn_expert_w, L0_ffn_expert_b):
    import jax
    import jax.numpy as jnp

    def _L0_cond_ref(initial_state, inputs, W_ih, W_hh, b_ih, b_hh):
        import jax, jax.numpy as jnp
        import numpy as np
        B, T, D = (16, 128, 512)
        "ScanOverTime(GRU cell): sequential per-timestep module call with\n            dict-state passing; merge_dict_trees stacks the per-step\n            'state_predicted' tensors along axis=1 -> [B, T, D]."

        def cell(h, x):
            gi = x @ W_ih + b_ih
            gh = h @ W_hh + b_hh
            i_r, i_z, i_n = jnp.split(gi, 3, axis=-1)
            h_r, h_z, h_n = jnp.split(gh, 3, axis=-1)
            r = jax.nn.sigmoid(i_r + h_r)
            z = jax.nn.sigmoid(i_z + h_z)
            n = jnp.tanh(i_n + r * h_n)
            h_new = (1.0 - z) * n + z * h
            return (h_new, h_new)
        xs = jnp.swapaxes(inputs, 0, 1)
        _, hs = jax.lax.scan(cell, initial_state, xs)
        return jnp.swapaxes(hs, 0, 1)

    def _L0_ffn_ref(x, router_w, router_b, expert_w, expert_b):
        import jax, jax.numpy as jnp
        import numpy as np
        NUM_EXPERTS = 16
        C = 1.0
        b, s, h = x.shape
        bs = b * s
        k = min(int(bs * C / NUM_EXPERTS), bs)
        xf = x.reshape(bs, h)
        logits = xf @ router_w + router_b
        S = jax.nn.softmax(logits, axis=-1)
        G, idx = jax.lax.top_k(S.T, k)
        tokens = xf[idx]
        out = jnp.einsum('ekh,hd->ekd', tokens, expert_w) + expert_b
        weighted = G[..., None] * out
        y = jnp.zeros((bs, h), dtype=x.dtype).at[idx.reshape(-1)].add(weighted.reshape(-1, h))
        return y.reshape(b, s, h)
    x = x + _L0_ffn_ref(_L0_cond_ref(cond_2048, x, L0_cond_W_ih, L0_cond_W_hh, L0_cond_b_ih, L0_cond_b_hh), L0_ffn_router_w, L0_ffn_router_b, L0_ffn_expert_w, L0_ffn_expert_b)
    return x

_drawn_inputs = setup_inputs


def setup_inputs(seed=0):
    import zlib

    import numpy as np

    out = dict(_drawn_inputs(seed))
    spreads = {'L0_cond_b_ih': (0.0, 0.8),
     'L0_cond_b_hh': (0.0, 0.8),
     'L0_ffn_router_b': (0.0, 0.8),
     'L0_ffn_expert_b': (0.0, 0.718)}
    factors = {'cond_2048': 8.0, 'L0_cond_W_hh': 4.561, 'L0_ffn_router_w': 3.627}
    for name, (base, spread) in spreads.items():
        noise = np.random.default_rng([zlib.crc32(name.encode()), seed]).standard_normal(out[name].shape)
        drawn = base * np.exp(spread * noise) if base else spread * noise
        out[name] = jnp.asarray(drawn.astype(out[name].dtype))
    for name, factor in factors.items():
        out[name] = (out[name] * factor).astype(out[name].dtype)
    return out
```

```python
import concourse.bass as bass
from concourse import mybir
from contextlib import ExitStack


def gru_expert_choice_kernel(nc, x, cond, w_ih, w_hh, b_ih, b_hh, router_w, router_b, expert_w, expert_b, out):
    F32, I32 = mybir.dt.float32, mybir.dt.int32
    ALU = mybir.AluOpType
    ACT = mybir.ActivationFunctionType
    AX = mybir.AxisListType

    B, T, D = x.shape
    NE = router_w.shape[1]
    P = 128
    Q = 32
    J = P // Q
    K = D // P
    G = 3
    TT = P // B
    NT = T // TT
    BODY = 2 * TT
    TURNS = T // BODY
    CAP = (B * T) // NE
    NG = 4
    NI = NT // NG
    XS = 24
    PH = 8
    HALF = (slice(0, K // 2), slice(K // 2, K))

    x_tiles = x.rearrange("b (i t) d -> i t b d", t=TT)
    x_phases = x.rearrange("b (h i t) d -> h t b i d", t=TT, i=PH)
    out_tiles = out.rearrange("b (i t) d -> i t b d", t=TT)

    ctx = ExitStack()
    with ctx:
        def sb(name, shape, dt=F32):
            return ctx.enter_context(nc.sbuf_tensor(name, shape, dt))

        def pb(name, shape):
            return ctx.enter_context(nc.psum_tensor(name, shape, F32))

        def sem(name):
            return ctx.enter_context(nc.semaphore(name))

        whh = sb("whh", [P, K, G * D])
        wih = sb("wih", [P, K, G * D])
        we = sb("we", [P, K, D])
        wr = sb("wr", [P, K, NE])
        be = sb("be", [P, D])
        br = sb("br", [P, NE])
        b_rows = sb("b_rows", [P, 2, Q])
        b_cols = sb("b_cols", [P, 2, Q])
        gate_bias = sb("gate_bias", [P, G, K])
        hn_bias = sb("hn_bias", [P, K, B])
        zeros = sb("zeros", [P, B])
        ident = sb("ident", [P, P])
        x_in = sb("x_in", [P, 2, D])
        xT = sb("xT", [P, K, P])
        giT = sb("giT", [P, 2, G, K, P])
        h0 = sb("h0", [P, P])
        hist = sb("hist", [P, 2, K, P])
        raw = sb("raw", [P, G, P])
        pre_r = sb("pre_r", [P, K, B])
        pre_z = sb("pre_z", [P, K, B])
        th_r = sb("th_r", [P, K, B])
        th_z = sb("th_z", [P, K, B])
        half_h = sb("half_h", [P, K, B])
        hnb = sb("hnb", [P, K, B])
        rh = sb("rh", [P, K, B])
        pre_n = sb("pre_n", [P, K, B])
        n_t = sb("n_t", [P, K, B])
        zh = sb("zh", [P, K, B])
        nz = sb("nz", [P, K, B])
        ffn = sb("ffn", [P, NT, D])
        logits = sb("logits", [P, NT, NE])
        xs = sb("xs", [P, XS, D])
        free = [wih[:, c // 3, (c % 3) * D:(c % 3 + 1) * D] for c in range(3 * K)]
        scores = logits[:, :, :]
        S, chosen, above, tie, prefix, rank, zeros_w, junk = (free[c] for c in range(8))
        scores_g = free[8].rearrange("p (g n) -> p g n", g=NG)
        same_expert = sb("same_expert", [P, P])
        before = sb("before", [P, P])
        group_of = sb("group_of", [P, NI])
        row = sb("row", [P, NT])
        row_inv = sb("row_inv", [P, NT])
        thr = sb("thr", [P, 1], I32)
        cand = sb("cand", [P, 1], I32)
        bit = sb("bit", [P, 1], I32)
        nbit = sb("nbit", [P, 1], I32)
        kept = sb("kept", [P, 1], I32)
        cnt = sb("cnt", [P, 1])
        need = sb("need", [P, 1])
        R = sb("R", [P, B])
        others = sb("others", [P, B])
        scan_b = sb("scan_b", [P, B])
        offset = sb("offset", [P, B])
        weight = sb("weight", [P, NG, NI])

        gh_ps = pb("gh_ps", [P, G, P])
        xT_ps = pb("xT_ps", [P, K, P])
        gi_ps = [pb(f"gi_ps{g}", [P, K, P]) for g in range(G)]
        ffn_ps = pb("ffn_ps", [P, D])
        log_ps = pb("log_ps", [P, NE])
        cnt_ps = pb("cnt_ps", [P, 4 * B])

        w_early = sem("w_early")
        w_late = sem("w_late")
        start_zeroed = sem("start_zeroed")
        h0_loaded = sem("h0_loaded")
        h0_turned = sem("h0_turned")
        ident_cleared = sem("ident_cleared")
        masks_step = sem("masks_step")
        masks_ready = sem("masks_ready")
        b_turned = sem("b_turned")
        bias_ready = sem("bias_ready")
        x_loaded = [sem(f"x_loaded{p}") for p in range(2)]
        xT_done = sem("xT_done")
        xT_ready = sem("xT_ready")
        gi_done = [sem(f"gi_done{g}") for g in range(G)]
        giT_ready = [sem(f"giT_ready{g}") for g in range(G)]
        gh_done = sem("gh_done")
        h_ready = [sem(f"h_ready{a}") for a in range(2)]
        raw_r = [sem(f"raw_r{a}") for a in range(2)]
        raw_z = sem("raw_z")
        raw_n = [sem(f"raw_n{a}") for a in range(2)]
        pre_r_ready = [sem(f"pre_r_ready{a}") for a in range(2)]
        pre_z_ready = sem("pre_z_ready")
        th_r_ready = [sem(f"th_r_ready{a}") for a in range(2)]
        th_z_ready = sem("th_z_ready")
        hnb_ready = [sem(f"hnb_ready{a}") for a in range(2)]
        rh_ready = [sem(f"rh_ready{a}") for a in range(2)]
        pre_n_ready = [sem(f"pre_n_ready{a}") for a in range(2)]
        n_ready = [sem(f"n_ready{a}") for a in range(2)]
        half_h_ready = sem("half_h_ready")
        nz_ready = [sem(f"nz_ready{a}") for a in range(2)]
        ffn_done = sem("ffn_done")
        ffn_stored = sem("ffn_stored")
        log_done = sem("log_done")
        log_stored = sem("log_stored")
        soft = sem("soft")
        soft_exp = sem("soft_exp")
        shifted = sem("shifted")
        scores_ready = sem("scores_ready")
        ST_done = sem("ST_done")
        S_ready = sem("S_ready")
        cand_ready = sem("cand_ready")
        cnt_own = sem("cnt_own")
        cnt_ready = sem("cnt_ready")
        cnt_all = sem("cnt_all")
        kept_ready = sem("kept_ready")
        bit_ready = sem("bit_ready")
        R_ready = sem("R_ready")
        R_summed = sem("R_summed")
        chosen_ready = sem("chosen_ready")
        weight_done = sem("weight_done")
        weight_ready = sem("weight_ready")
        xs_loaded = [sem(f"xs_loaded{p}") for p in range(NT // PH)]
        out_ready = sem("out_ready")
        stored = sem("stored")

        block = ctx.enter_context(nc.Block())

        @block.sync
        def _(sp):
            def load_x(n, parity):
                sp.dma_start(x_in[:, parity, :], x_tiles[n]).then_inc(x_loaded[parity], 16)

            load_x(0, 0)
            load_x(1, 1)
            for kc in range(K):
                sp.dma_start(wih[:, kc, :], w_ih[kc * P:(kc + 1) * P, :]).then_inc(w_early, 16)
            for k in range(K):
                sp.dma_start(we[:, k, :], expert_w[k * P:(k + 1) * P, :]).then_inc(w_late, 16)
                sp.dma_start(wr[:, k, :], router_w[k * P:(k + 1) * P, :]).then_inc(w_late, 16)
            sp.dma_start(be[:, :], expert_b.partition_broadcast(P)).then_inc(w_late, 16)
            sp.dma_start(br[:, :], router_b.partition_broadcast(P)).then_inc(w_late, 16)
            with sp.Fori(0, NT // 2 - 1) as m:
                for parity in range(2):
                    sp.wait_ge(xT_done, m * 2 + parity + 1)
                    load_x(m * 2 + parity + 2, parity)
            for ph in range(NT // PH):
                first_slot = ph * PH % XS
                if ph * PH >= XS:
                    sp.wait_ge(out_ready, ph * PH - XS + PH)
                for tt in range(TT):
                    sp.dma_start(xs[tt * B:(tt + 1) * B, first_slot:first_slot + PH, :],
                                 x_phases[ph, tt]).then_inc(xs_loaded[ph], 16)
            with sp.Fori(0, NT // 2) as m:
                sp.wait_ge(out_ready, m * 2 + 1)
                sp.dma_start(out_tiles[m * 2], ffn[:, m * 2, :]).then_inc(stored, 16)
            sp.wait_ge(stored, NT * 16)

        @block.gpsimd
        def _(pool):
            step = 0

            def select(out_, pattern, op, fill_, base, mult):
                nonlocal step
                if step:
                    pool.wait_ge(masks_step, step)
                step += 1
                nc.gpsimd.affine_select(out=out_, in_=out_, pattern=pattern, compare_op=op, fill=fill_,
                                        base=base, channel_multiplier=mult).then_inc(masks_step, 1)

            nc.gpsimd.memset(ident[:, :], 0.0).then_inc(ident_cleared, 1)
            nc.gpsimd.memset(same_expert[:, :], 0.0).then_inc(ident_cleared, 1)
            nc.gpsimd.memset(group_of[:, :], 1.0).then_inc(ident_cleared, 1)
            pool.wait_ge(ident_cleared, 3)
            select(ident[:, :], [[-1, P]], ALU.not_equal, 1.0, 0, 1)
            for i in range(NI):
                select(same_expert[:, :], [[0, NI], [-1, NE]], ALU.not_equal, 1.0, -NE * i, 1)
            select(group_of[:, :], [[-NE, NI]], ALU.is_ge, 0.0, 0, 1)
            select(group_of[:, :], [[NE, NI]], ALU.is_ge, 0.0, NE - 1, -1)
            pool.wait_ge(masks_step, step)
            nc.gpsimd.tensor_copy(before[:, :], same_expert[:, :]).then_inc(masks_step, 1)
            step += 1
            select(before[:, :], [[1, P]], ALU.is_gt, 0.0, 0, -1)
            pool.wait_ge(masks_step, step)
            nc.gpsimd.memset(zeros[:, :], 0.0).then_inc(masks_ready, 1)

        @block.scalar
        def _(act):
            act.wait_ge(start_zeroed, 1)
            for j in range(J):
                for n, b in enumerate((b_ih, b_hh)):
                    act.dma_start(b_rows[Q * j:Q * j + G * K, n, :],
                                  b.rearrange("(r j c) -> j r c", j=J, c=Q)[j]).then_inc(w_early, 16)
            for k in range(K):
                act.dma_start(whh[:, k, :], w_hh[k * P:(k + 1) * P, :]).then_inc(w_late, 16)
            for j in range(J):
                act.dma_start(h0[Q * j:Q * j + B, :],
                              cond.rearrange("b (k j c) -> j b k c", j=J, c=Q)[j]).then_inc(h0_loaded, 16)

            def evacuate_xT(n):
                act.wait_ge(xT_done, n + 1)
                nc.scalar.activation(xT[:, :, :], xT_ps[:, :, :], ACT.Copy).then_inc(xT_ready, 1)

            def evacuate_gi(n, parity, g):
                act.wait_ge(gi_done[g], n + 1)
                for k in range(K):
                    last = nc.scalar.activation(giT[:, parity, g, k, :], gi_ps[g][:, k, :], ACT.Identity,
                                                bias=gate_bias[:, g, k:k + 1])
                last.then_inc(giT_ready[g], 1)

            def tanh_r(t, a):
                act.wait_ge(pre_r_ready[a], t + 1)
                nc.scalar.activation(th_r[:, HALF[a], :], pre_r[:, HALF[a], :], ACT.Tanh,
                                     scale=0.5).then_inc(th_r_ready[a], 1)

            def tanh_z(t):
                act.wait_ge(pre_z_ready, t + 1)
                nc.scalar.activation(th_z[:, :, :], pre_z[:, :, :], ACT.Tanh, scale=0.5).then_inc(th_z_ready, 1)

            def tanh_n(t, a):
                act.wait_ge(pre_n_ready[a], t + 1)
                nc.scalar.activation(n_t[:, HALF[a], :], pre_n[:, HALF[a], :], ACT.Tanh).then_inc(n_ready[a], 1)

            def turn(m, first, last):
                for par in range(2):
                    i = m * 2 + par
                    for s in range(TT):
                        t = m * BODY + (par * TT + s)
                        has_next = not (last and par == 1)
                        if s == 0 and not (first and par == 0):
                            evacuate_gi(i, par, 2)
                        if s == 1 and has_next:
                            evacuate_xT(i + 1)
                        if s == 5 and has_next:
                            evacuate_gi(i + 1, 1 - par, 0)
                        if s == 7 and has_next:
                            evacuate_gi(i + 1, 1 - par, 1)
                        tanh_r(t, 0)
                        tanh_z(t)
                        tanh_n(t, 0)
                        tanh_r(t, 1)
                        tanh_n(t, 1)

            evacuate_xT(0)
            act.wait_ge(bias_ready, 1)
            for g in range(G):
                evacuate_gi(0, 0, g)
            turn(0, True, False)
            with act.Fori(1, TURNS - 1) as m:
                turn(m, False, False)
            turn(TURNS - 1, False, True)
            act.wait_ge(shifted, 1)
            nc.scalar.activation(scores, scores, ACT.Exp).then_inc(soft_exp, 1)
            with act.Fori(0, NT // 2) as m:
                act.wait_ge(out_ready, m * 2 + 2)
                act.dma_start(out_tiles[m * 2 + 1], ffn[:, m * 2 + 1, :]).then_inc(stored, 16)

        @block.tensor
        def _(pe):
            def transpose_x(n, parity, loads):
                pe.wait_ge(x_loaded[parity], loads)
                for kc in range(K):
                    mm = nc.tensor.transpose(xT_ps[:, kc, :], x_in[:, parity, kc * P:(kc + 1) * P], ident[:, :])
                mm.then_inc(xT_done, 1)

            def project(n, g, k, kc, prior):
                if g == 0 and k == 0 and kc == 0:
                    pe.wait_ge(xT_ready, n + 1)
                if k == 0 and kc == 0 and prior:
                    pe.wait_ge(giT_ready[g], n)
                first = g * D + k * P
                mm = nc.tensor.matmul(gi_ps[g][:, k, :], wih[:, kc, first:first + P], xT[:, kc, :], start=(kc == 0), stop=(kc == K - 1),
                                      skip_group_check=True)
                if k == K - 1 and kc == K - 1:
                    mm.then_inc(gi_done[g], 1)

            def expert(n, par, k, prior):
                if k == 0 and prior:
                    pe.wait_ge(ffn_stored, n)
                mm = nc.tensor.matmul(ffn_ps[:, :], hist[:, par, k, :], we[:, k, :], start=(k == 0), stop=(k == K - 1))
                if k == K - 1:
                    mm.then_inc(ffn_done, 1)

            def router(n, par, prior):
                if prior:
                    pe.wait_ge(log_stored, n)
                for k in range(K):
                    mm = nc.tensor.matmul(log_ps[:, :], hist[:, par, k, :], wr[:, k, :], start=(k == 0), stop=(k == K - 1))
                mm.then_inc(log_done, 1)

            def recurrent(t, par, s):
                hp, hs = (par, s - 1) if s else (1 - par, TT - 1)
                for k in range(K):
                    if k % (K // 2) == 0:
                        pe.wait_ge(h_ready[k // (K // 2)], t + 1)
                    for j in range(J):
                        mm = nc.tensor.matmul(
                            gh_ps[Q * j:Q * j + B, :, :].rearrange("b g (k c) -> b (g k) c", c=Q),
                            hist[:, hp, k, hs * B:(hs + 1) * B],
                            whh[:, k, :].rearrange("p (r j c) -> p j r c", j=J, c=Q)[:, j],
                            start=(k == 0), stop=(k == K - 1))
                mm.then_inc(gh_done, 1)

            GI = [(g, k, kc) for g in range(G) for k in range(K) for kc in range(K)]
            GI_STEPS = [0, 4, 4, 4, 9, 9, 9, 9]

            def turn(m, first, last):
                for par in range(2):
                    i = m * 2 + par
                    has_next = not (last and par == 1)
                    has_prior = not (first and par == 0)
                    at = 0
                    for s in range(TT):
                        recurrent(m * BODY + (par * TT + s), par, s)
                        if s == 0 and has_next:
                            transpose_x(i + 1, 1 - par, (m + par) * 16 + 16)
                        if s < K and has_prior:
                            expert(i - 1, 1 - par, s, not (first and par == 1))
                        if s == 0 and has_prior:
                            router(i - 1, 1 - par, not (first and par == 1))
                        if has_next:
                            for g, k, kc in GI[at:at + GI_STEPS[s]]:
                                project(i + 1, g, k, kc, True)
                            at += GI_STEPS[s]

            pe.wait_ge(masks_ready, 1)
            transpose_x(0, 0, 16)
            pe.wait_ge(w_early, (K + 2 * J) * 16)
            for g, k, kc in GI:
                project(0, g, k, kc, False)
            pe.wait_ge(w_late, (3 * J + 2) * 16)
            turn(0, True, False)
            with pe.Fori(1, TURNS - 1) as m:
                turn(m, False, False)
            turn(TURNS - 1, False, True)
            pe.wait_ge(h_ready[0], T + 1)
            pe.wait_ge(h_ready[1], T + 1)
            router(NT - 1, 1, True)
            for k in range(K):
                expert(NT - 1, 1, k, True)
            pe.wait_ge(scores_ready, 1)
            for g in range(NG):
                mm = nc.tensor.transpose(xT_ps[:, g, :],
                                         scores_g[:, g, :], ident[:, :])
            mm.then_inc(ST_done, 1)
            with pe.Fori(0, 30) as r:
                pe.wait_ge(cnt_own, r + 1)
                nc.tensor.matmul(cnt_ps[:, 0:1], same_expert[:, :], cnt[:, :], start=True, stop=True).then_inc(cnt_all, 1)
            pe.wait_ge(cnt_own, 31)
            nc.tensor.matmul(cnt_ps[:, 0:1], same_expert[:, :], cnt[:, :], start=True, stop=True).then_inc(cnt_all, 1)
            pe.wait_ge(R_ready, 1)
            nc.tensor.matmul(gi_ps[0][:, 0, 0:B], same_expert[:, :], R[:, :], start=True, stop=True)
            nc.tensor.matmul(gi_ps[1][:, 0, 0:B], before[:, :], R[:, :], start=True, stop=True).then_inc(R_summed, 1)
            pe.wait_ge(chosen_ready, 1)
            for g in range(NG):
                mm = nc.tensor.matmul(gi_ps[2][:, 0, g * NI:(g + 1) * NI],
                                      chosen[:, g * P:(g + 1) * P],
                                      group_of[:, :], start=True, stop=True, skip_group_check=True)
            mm.then_inc(weight_done, 1)

        @block.vector
        def _(dve):
            V = nc.vector
            V.memset(b_rows[:, :, :], 0.0)
            V.memset(h0[:, :], 0.0).then_inc(start_zeroed, 1)
            V.memset(gh_ps[:, :, :], 0.0)
            dve.wait_ge(w_early, (K + 2 * J) * 16)
            V.transpose(b_cols[:, :, :], b_rows[:, :, :]).then_inc(b_turned, 1)
            dve.wait_ge(b_turned, 1)
            bi, bh = (b_cols[:, n, 0:G * K].rearrange("p (g k) -> p g k", g=G) for n in range(2))
            V.tensor_tensor(gate_bias[:, 0:2, :], bi[:, 0:2, :], bh[:, 0:2, :], ALU.add)
            V.tensor_copy(gate_bias[:, 2, :], bi[:, 2, :]).then_inc(bias_ready, 1)
            dve.wait_ge(masks_ready, 1)
            for k in range(K):
                V.tensor_scalar(hn_bias[:, k, :], zeros[:, :], bh[:, 2, k:k + 1], 0.5, ALU.add, ALU.mult)
            dve.wait_ge(h0_loaded, J * 16)
            V.transpose(raw[:, 0, :], h0[:, :]).then_inc(h0_turned, 1)
            dve.wait_ge(h0_turned, 1)
            first_state = raw[:, 0, :].rearrange("p (k q) -> p k q", q=Q)[:, :, 0:B]
            V.tensor_scalar(half_h[:, :, :], first_state, 0.5, None, ALU.mult).then_inc(half_h_ready, 1)
            for a in range(2):
                V.tensor_copy(hist[:, 1, HALF[a], (TT - 1) * B:TT * B], first_state[:, HALF[a]]).then_inc(h_ready[a], 1)
            dve.wait_ge(w_late, (3 * J + 2) * 16)

            raw_k = raw[:, :, :].rearrange("p g (k q) -> p g k q", q=Q)

            def step(t, par, s):
                cols = slice(s * B, (s + 1) * B)

                def turned(gate, half, done):
                    V.transpose(raw[:, gate, half], gh_ps[:, gate, half]).then_inc(done, 1)

                def add_gi_r(a):
                    dve.wait_ge(raw_r[a], t + 1)
                    V.tensor_tensor(pre_r[:, HALF[a], :], raw_k[:, 0, HALF[a], 0:B], giT[:, par, 0, HALF[a], cols],
                                    ALU.add).then_inc(pre_r_ready[a], 1)

                def add_gi_z():
                    dve.wait_ge(raw_z, t + 1)
                    V.tensor_tensor(pre_z[:, :, :], raw_k[:, 1, :, 0:B], giT[:, par, 1, :, cols],
                                    ALU.add).then_inc(pre_z_ready, 1)

                def add_hn_bias(a):
                    dve.wait_ge(raw_n[a], t + 1)
                    V.scalar_tensor_tensor(hnb[:, HALF[a], :], raw_k[:, 2, HALF[a], 0:B], 0.5, hn_bias[:, HALF[a], :],
                                           ALU.mult, ALU.add).then_inc(hnb_ready[a], 1)

                def reset_hn(a):
                    dve.wait_ge(th_r_ready[a], t + 1)
                    V.scalar_tensor_tensor(rh[:, HALF[a], :], th_r[:, HALF[a], :], 1.0, hnb[:, HALF[a], :],
                                           ALU.add, ALU.mult).then_inc(rh_ready[a], 1)

                def add_gi_n(a):
                    dve.wait_ge(rh_ready[a], t + 1)
                    V.tensor_tensor(pre_n[:, HALF[a], :], rh[:, HALF[a], :], giT[:, par, 2, HALF[a], cols],
                                    ALU.add).then_inc(pre_n_ready[a], 1)

                def z_times_h(a):
                    dve.wait_ge(th_z_ready, t + 1)
                    V.scalar_tensor_tensor(zh[:, HALF[a], :], th_z[:, HALF[a], :], 1.0, half_h[:, HALF[a], :],
                                           ALU.add, ALU.mult)

                def n_part(a):
                    dve.wait_ge(n_ready[a], t + 1)
                    V.scalar_tensor_tensor(nz[:, HALF[a], :], th_z[:, HALF[a], :], 1.0, n_t[:, HALF[a], :],
                                           ALU.subtract, ALU.mult).then_inc(nz_ready[a], 1)

                def new_state(a):
                    dve.wait_ge(nz_ready[a], t + 1)
                    V.scalar_tensor_tensor(hist[:, par, HALF[a], cols], nz[:, HALF[a], :], -0.5, zh[:, HALF[a], :],
                                           ALU.mult, ALU.add).then_inc(h_ready[a], 1)

                dve.wait_ge(gh_done, t + 1)
                turned(0, slice(0, P // 2), raw_r[0])
                turned(2, slice(0, P // 2), raw_n[0])
                add_gi_r(0)
                add_hn_bias(0)
                turned(1, slice(0, P), raw_z)
                dve.wait_ge(hnb_ready[0], t + 1)
                turned(0, slice(P // 2, P), raw_r[1])
                reset_hn(0)
                add_gi_z()
                add_gi_n(0)
                add_gi_r(1)
                turned(2, slice(P // 2, P), raw_n[1])
                z_times_h(0)
                n_part(0)
                add_hn_bias(1)
                new_state(0)
                dve.wait_ge(hnb_ready[1], t + 1)
                reset_hn(1)
                z_times_h(1)
                add_gi_n(1)
                n_part(1)
                new_state(1)
                dve.wait_ge(h_ready[1], t + 2)
                V.tensor_scalar(half_h[:, :, :], hist[:, par, :, cols], 0.5, None, ALU.mult).then_inc(half_h_ready, 1)

            def store_logits(n):
                dve.wait_ge(log_done, n + 1)
                V.tensor_tensor(logits[:, n, :], log_ps[:, :], br[:, :], ALU.add).then_inc(log_stored, 1)

            def store_ffn(n, c):
                half = slice(c * D // 2, (c + 1) * D // 2)
                if c == 0:
                    dve.wait_ge(ffn_done, n + 1)
                ins = V.tensor_tensor(ffn[:, n, half], ffn_ps[:, half], be[:, half], ALU.add)
                if c == 1:
                    ins.then_inc(ffn_stored, 1)

            def turn(m, first, last):
                for par in range(2):
                    i = m * 2 + par
                    for g in range(G):
                        dve.wait_ge(giT_ready[g], i + 1)
                    for s in range(TT):
                        step(m * BODY + (par * TT + s), par, s)
                        if not (first and par == 0):
                            if s == 1:
                                store_logits(i - 1)
                            if s in (4, 5):
                                store_ffn(i - 1, s - 4)

            turn(0, True, False)
            with dve.Fori(1, TURNS - 1) as m:
                turn(m, False, False)
            turn(TURNS - 1, False, True)
            store_logits(NT - 1)

            chain = 0

            def link(ins):
                nonlocal chain
                chain += 1
                ins.then_inc(soft, 1)
                dve.wait_ge(soft, chain)

            dve.wait_ge(log_stored, NT)
            link(V.tensor_reduce(row[:, :], scores, AX.X, ALU.max))
            V.tensor_tensor(scores, scores, row[:, :].unsqueeze(2).broadcast_to([P, NT, NE]), ALU.subtract)\
                .then_inc(shifted, 1)
            store_ffn(NT - 1, 0)
            store_ffn(NT - 1, 1)
            V.memset(zeros_w, 0.0)
            V.memset(thr[:, :], 0)
            V.memset(cand[:, :], 1 << 29)
            V.memset(bit[:, :], 1 << 29)
            dve.wait_ge(soft_exp, 1)
            link(V.tensor_reduce(row[:, :], scores, AX.X, ALU.add))
            link(V.reciprocal(row_inv[:, :], row[:, :]))
            V.tensor_tensor(scores_g.rearrange("p g (i e) -> p i g e", i=NI),
                            scores.rearrange("p (i g) e -> p i g e", g=NG),
                            row_inv[:, :].rearrange("p (i g) -> p i g", g=NG).unsqueeze(3).broadcast_to([P, NI, NG, NE]),
                            ALU.mult)\
                .then_inc(scores_ready, 1)
            dve.wait_ge(ST_done, 1)
            link(V.tensor_copy(S.rearrange("p (b g t) -> p b g t", b=B, g=NG),
                               xT_ps[:, :, :].rearrange("p g (t b) -> p b g t", b=B)))

            with dve.Fori(0, 30) as r:
                V.tensor_scalar(junk, S, cand[:, :].bitcast(F32), None, ALU.is_ge, ALU.add,
                                accum_out=cnt[:, :]).then_inc(cnt_own, 1)
                V.tensor_scalar(nbit[:, :], bit[:, :], 1, None, ALU.logical_shift_right).then_inc(bit_ready, 1)
                dve.wait_ge(cnt_all, r + 1)
                V.scalar_tensor_tensor(kept[:, :], cnt_ps[:, 0:1], float(CAP), bit[:, :], ALU.is_ge, ALU.mult)\
                    .then_inc(kept_ready, 1)
                dve.wait_ge(bit_ready, r + 1)
                dve.wait_ge(kept_ready, r + 1)
                V.tensor_tensor(thr[:, :], thr[:, :], kept[:, :], ALU.bitwise_or).then_inc(cand_ready, 1)
                V.tensor_copy(bit[:, :], nbit[:, :]).then_inc(cand_ready, 1)
                dve.wait_ge(cand_ready, r * 3 + 2)
                V.tensor_tensor(cand[:, :], thr[:, :], nbit[:, :], ALU.bitwise_or).then_inc(cand_ready, 1)
                dve.wait_ge(cand_ready, r * 3 + 3)
            thr_f = thr[:, :].bitcast(F32)
            V.tensor_scalar(above, S, thr_f, None, ALU.is_gt, ALU.add, accum_out=cnt[:, :]).then_inc(cnt_own, 1)
            link(V.tensor_scalar(tie, S, thr_f, None, ALU.is_equal))
            V.tensor_reduce(R[:, :], tie.rearrange("p (b n) -> p b n", b=B), AX.X, ALU.add).then_inc(R_ready, 1)
            link(V.tensor_tensor_scan(prefix, tie, zeros_w, 0.0, ALU.add, ALU.add))
            dve.wait_ge(cnt_all, 31)
            V.tensor_scalar(need[:, :], cnt_ps[:, 0:1], -1.0, float(CAP), ALU.mult, ALU.add)
            dve.wait_ge(R_ready, 1)
            dve.wait_ge(R_summed, 1)
            link(V.tensor_tensor(others[:, :], gi_ps[0][:, 0, 0:B], R[:, :], ALU.subtract))
            link(V.tensor_tensor_scan(scan_b[:, :], others[:, :], zeros[:, :], 0.0, ALU.add, ALU.add))
            link(V.tensor_tensor(offset[:, :], scan_b[:, :], others[:, :], ALU.subtract))
            link(V.tensor_tensor(offset[:, :], gi_ps[1][:, 0, 0:B], offset[:, :], ALU.add))
            link(V.tensor_tensor(rank.rearrange("p (b n) -> p b n", b=B), prefix.rearrange("p (b n) -> p b n", b=B),
                                 offset[:, :].unsqueeze(2).broadcast_to([P, B, NG * TT]), ALU.add))
            link(V.scalar_tensor_tensor(rank, rank, need[:, :], tie, ALU.is_le, ALU.mult))
            link(V.tensor_tensor(above, above, rank, ALU.add))
            by_token = "p (b g t) -> p b g t"
            V.tensor_tensor(chosen.rearrange("p (g t b) -> p b g t", g=NG, b=B), S.rearrange(by_token, b=B, g=NG),
                            above.rearrange(by_token, b=B, g=NG), ALU.mult).then_inc(chosen_ready, 1)
            dve.wait_ge(weight_done, 1)
            link(V.tensor_copy(weight[:, :, :], gi_ps[2][:, 0, 0:NG * NI].rearrange("p (g i) -> p g i", g=NG)))
            dve.wait_ge(ffn_stored, NT)
            for ph in range(NT // PH):
                dve.wait_ge(xs_loaded[ph], TT * 16)
                for o in range(PH):
                    n = ph * PH + o
                    V.scalar_tensor_tensor(ffn[:, n, :], ffn[:, n, :], weight[:, n % NG, n // NG:n // NG + 1],
                                           xs[:, n % XS, :], ALU.mult, ALU.add).then_inc(out_ready, 1)


_INS = ["x", "cond_2048", "L0_cond_W_ih", "L0_cond_W_hh", "L0_cond_b_ih", "L0_cond_b_hh", "L0_ffn_router_w",
        "L0_ffn_router_b", "L0_ffn_expert_w", "L0_ffn_expert_b"]


def kernel(**inputs):
    import numpy as _np
    import concourse.bacc as _bacc
    from concourse import mybir as _mybir
    from concourse.bass_utils import run_bass_kernel_spmd as _run

    nc = _bacc.Bacc("TRN2", target_bir_lowering=False, num_devices=1)
    arrays, args = {}, []
    for name in _INS:
        a = _np.ascontiguousarray(inputs[name])
        arrays[f"in_{name}"] = a
        args.append(nc.dram_tensor(f"in_{name}", a.shape, _mybir.dt.from_np(a.dtype), kind="ExternalInput").ap())
    shape = inputs["x"].shape
    args.append(nc.dram_tensor("out", shape, _mybir.dt.from_np(_np.dtype("float32")), kind="ExternalOutput").ap())
    gru_expert_choice_kernel(nc, *args)
    r = _run(nc, [arrays], core_ids=[0])
    return r.results[0]["out"]
```

```python
import concourse.bass as bass
from concourse import mybir
from contextlib import ExitStack


def gru_expert_choice_kernel(nc, x, cond, w_ih, w_hh, b_ih, b_hh, router_w, router_b, expert_w, expert_b, out):
    F32, I32 = mybir.dt.float32, mybir.dt.int32
    ALU = mybir.AluOpType
    ACT = mybir.ActivationFunctionType
    AX = mybir.AxisListType

    B, T, D = x.shape
    NE = router_w.shape[1]
    P = 128
    Q = 32
    J = P // Q
    K = D // P
    G = 3
    TT = P // B
    NT = T // TT
    BODY = 2 * TT
    TURNS = T // BODY
    CAP = (B * T) // NE
    NG = 4
    NI = NT // NG
    TOP_BIT = 29
    ROUNDS = (TOP_BIT + 1) // 2
    XS = 24
    PH = 8
    HALF = (slice(0, K // 2), slice(K // 2, K))

    x_tiles = x.rearrange("b (i t) d -> i t b d", t=TT)
    x_phases = x.rearrange("b (h i t) d -> h t b i d", t=TT, i=PH)
    out_tiles = out.rearrange("b (i t) d -> i t b d", t=TT)

    ctx = ExitStack()
    with ctx:
        def sb(name, shape, dt=F32):
            return ctx.enter_context(nc.sbuf_tensor(name, shape, dt))

        def pb(name, shape):
            return ctx.enter_context(nc.psum_tensor(name, shape, F32))

        def sem(name):
            return ctx.enter_context(nc.semaphore(name))

        whh = sb("whh", [P, K, G * D])
        wih = sb("wih", [P, K, G * D])
        we = sb("we", [P, K, D])
        wr = sb("wr", [P, K, NE])
        be = sb("be", [P, D])
        br = sb("br", [P, NE])
        b_rows = sb("b_rows", [P, 2, Q])
        b_cols = sb("b_cols", [P, 2, Q])
        gate_bias = sb("gate_bias", [P, G, K])
        hn_bias = sb("hn_bias", [P, K, B])
        zeros = sb("zeros", [P, B])
        ident = sb("ident", [P, P])
        x_in = sb("x_in", [P, 2, D])
        xT = sb("xT", [P, K, P])
        giT = sb("giT", [P, 2, G, K, P])
        h0 = sb("h0", [P, P])
        hist = sb("hist", [P, 2, K, P])
        raw = sb("raw", [P, G, P])
        pre_r = sb("pre_r", [P, K, B])
        pre_z = sb("pre_z", [P, K, B])
        th_r = sb("th_r", [P, K, B])
        th_z = sb("th_z", [P, K, B])
        half_h = sb("half_h", [P, K, B])
        hnb = sb("hnb", [P, K, B])
        rh = sb("rh", [P, K, B])
        pre_n = sb("pre_n", [P, K, B])
        n_t = sb("n_t", [P, K, B])
        zh = sb("zh", [P, K, B])
        nz = sb("nz", [P, K, B])
        ffn = sb("ffn", [P, NT, D])
        logits = sb("logits", [P, NT, NE])
        xs = sb("xs", [P, XS, D])
        free = [wih[:, c // 3, (c % 3) * D:(c % 3 + 1) * D] for c in range(3 * K)]
        scores = logits[:, :, :]
        S, chosen, above, tie, prefix, rank, zeros_w = (free[c] for c in range(7))
        junk = free[9:12]
        scores_g = free[8].rearrange("p (g n) -> p g n", g=NG)
        same_expert = sb("same_expert", [P, P])
        before = sb("before", [P, P])
        group_of = sb("group_of", [P, NI])
        row = sb("row", [P, NT])
        row_inv = sb("row_inv", [P, NT])
        thr = sb("thr", [P, 1], I32)
        cand = sb("cand", [P, 3], I32)
        steps = sb("steps", [P, 2, 3], I32)
        kept = sb("kept", [P, 1], I32)
        cnt = sb("cnt", [P, 3])
        reached = sb("reached", [P, 3])
        n_reached = sb("n_reached", [P, 1])
        need = sb("need", [P, 1])
        R = sb("R", [P, B])
        others = sb("others", [P, B])
        scan_b = sb("scan_b", [P, B])
        offset = sb("offset", [P, B])
        weight = sb("weight", [P, NG, NI])

        gh_ps = pb("gh_ps", [P, G, P])
        xT_ps = pb("xT_ps", [P, K, P])
        gi_ps = [pb(f"gi_ps{g}", [P, K, P]) for g in range(G)]
        ffn_ps = pb("ffn_ps", [P, D])
        log_ps = pb("log_ps", [P, NE])
        cnt_ps = pb("cnt_ps", [P, 4 * B])

        w_early = sem("w_early")
        w_late = sem("w_late")
        start_zeroed = sem("start_zeroed")
        h0_loaded = sem("h0_loaded")
        h0_turned = sem("h0_turned")
        ident_cleared = sem("ident_cleared")
        masks_step = sem("masks_step")
        masks_ready = sem("masks_ready")
        b_turned = sem("b_turned")
        bias_ready = sem("bias_ready")
        x_loaded = [sem(f"x_loaded{p}") for p in range(2)]
        xT_done = sem("xT_done")
        xT_ready = sem("xT_ready")
        gi_done = [sem(f"gi_done{g}") for g in range(G)]
        giT_ready = [sem(f"giT_ready{g}") for g in range(G)]
        gh_done = sem("gh_done")
        h_ready = [sem(f"h_ready{a}") for a in range(2)]
        raw_r = [sem(f"raw_r{a}") for a in range(2)]
        raw_z = [sem(f"raw_z{a}") for a in range(2)]
        raw_n = [sem(f"raw_n{a}") for a in range(2)]
        pre_r_ready = [sem(f"pre_r_ready{a}") for a in range(2)]
        pre_z_ready = [sem(f"pre_z_ready{a}") for a in range(2)]
        th_r_ready = [sem(f"th_r_ready{a}") for a in range(2)]
        th_z_ready = [sem(f"th_z_ready{a}") for a in range(2)]
        hnb_ready = [sem(f"hnb_ready{a}") for a in range(2)]
        rh_ready = [sem(f"rh_ready{a}") for a in range(2)]
        pre_n_ready = [sem(f"pre_n_ready{a}") for a in range(2)]
        n_ready = [sem(f"n_ready{a}") for a in range(2)]
        half_h_ready = sem("half_h_ready")
        nz_ready = [sem(f"nz_ready{a}") for a in range(2)]
        ffn_done = sem("ffn_done")
        ffn_stored = sem("ffn_stored")
        log_done = sem("log_done")
        log_stored = sem("log_stored")
        soft = sem("soft")
        soft_exp = sem("soft_exp")
        shifted = sem("shifted")
        scores_ready = sem("scores_ready")
        ST_done = sem("ST_done")
        S_ready = sem("S_ready")
        cand_ready = sem("cand_ready")
        cnt_own = sem("cnt_own")
        cnt_all = sem("cnt_all")
        kept_ready = sem("kept_ready")
        reached_ready = sem("reached_ready")
        R_ready = sem("R_ready")
        R_summed = sem("R_summed")
        chosen_ready = sem("chosen_ready")
        weight_done = sem("weight_done")
        weight_ready = sem("weight_ready")
        xs_loaded = [sem(f"xs_loaded{p}") for p in range(NT // PH)]
        out_ready = sem("out_ready")
        stored = sem("stored")

        block = ctx.enter_context(nc.Block())

        @block.sync
        def _(sp):
            def load_x(n, parity):
                sp.dma_start(x_in[:, parity, :], x_tiles[n]).then_inc(x_loaded[parity], 16)

            load_x(0, 0)
            load_x(1, 1)
            for kc in range(K):
                sp.dma_start(wih[:, kc, :], w_ih[kc * P:(kc + 1) * P, :]).then_inc(w_early, 16)
            for k in range(K):
                sp.dma_start(we[:, k, :], expert_w[k * P:(k + 1) * P, :]).then_inc(w_late, 16)
                sp.dma_start(wr[:, k, :], router_w[k * P:(k + 1) * P, :]).then_inc(w_late, 16)
            sp.dma_start(be[:, :], expert_b.partition_broadcast(P)).then_inc(w_late, 16)
            sp.dma_start(br[:, :], router_b.partition_broadcast(P)).then_inc(w_late, 16)
            with sp.Fori(0, NT // 2 - 1) as m:
                for parity in range(2):
                    sp.wait_ge(xT_done, m * 2 + parity + 1)
                    load_x(m * 2 + parity + 2, parity)
            for ph in range(NT // PH):
                first_slot = ph * PH % XS
                if ph * PH >= XS:
                    sp.wait_ge(out_ready, ph * PH - XS + PH)
                for tt in range(TT):
                    sp.dma_start(xs[tt * B:(tt + 1) * B, first_slot:first_slot + PH, :],
                                 x_phases[ph, tt]).then_inc(xs_loaded[ph], 16)
            with sp.Fori(0, NT // 2) as m:
                sp.wait_ge(out_ready, m * 2 + 1)
                sp.dma_start(out_tiles[m * 2], ffn[:, m * 2, :]).then_inc(stored, 16)
            sp.wait_ge(stored, NT * 16)

        @block.gpsimd
        def _(pool):
            step = 0

            def select(out_, pattern, op, fill_, base, mult):
                nonlocal step
                if step:
                    pool.wait_ge(masks_step, step)
                step += 1
                nc.gpsimd.affine_select(out=out_, in_=out_, pattern=pattern, compare_op=op, fill=fill_,
                                        base=base, channel_multiplier=mult).then_inc(masks_step, 1)

            nc.gpsimd.memset(ident[:, :], 0.0).then_inc(ident_cleared, 1)
            nc.gpsimd.memset(same_expert[:, :], 0.0).then_inc(ident_cleared, 1)
            nc.gpsimd.memset(group_of[:, :], 1.0).then_inc(ident_cleared, 1)
            pool.wait_ge(ident_cleared, 3)
            select(ident[:, :], [[-1, P]], ALU.not_equal, 1.0, 0, 1)
            for i in range(NI):
                select(same_expert[:, :], [[0, NI], [-1, NE]], ALU.not_equal, 1.0, -NE * i, 1)
            select(group_of[:, :], [[-NE, NI]], ALU.is_ge, 0.0, 0, 1)
            select(group_of[:, :], [[NE, NI]], ALU.is_ge, 0.0, NE - 1, -1)
            pool.wait_ge(masks_step, step)
            nc.gpsimd.tensor_copy(before[:, :], same_expert[:, :]).then_inc(masks_step, 1)
            step += 1
            select(before[:, :], [[1, P]], ALU.is_gt, 0.0, 0, -1)
            pool.wait_ge(masks_step, step)
            nc.gpsimd.memset(zeros[:, :], 0.0).then_inc(masks_ready, 1)

        @block.scalar
        def _(act):
            act.wait_ge(start_zeroed, 1)
            for j in range(J):
                for n, b in enumerate((b_ih, b_hh)):
                    act.dma_start(b_rows[Q * j:Q * j + G * K, n, :],
                                  b.rearrange("(r j c) -> j r c", j=J, c=Q)[j]).then_inc(w_early, 16)
            for k in range(K):
                act.dma_start(whh[:, k, :], w_hh[k * P:(k + 1) * P, :]).then_inc(w_late, 16)
            for j in range(J):
                act.dma_start(h0[Q * j:Q * j + B, :],
                              cond.rearrange("b (k j c) -> j b k c", j=J, c=Q)[j]).then_inc(h0_loaded, 16)

            def evacuate_xT(n):
                act.wait_ge(xT_done, n + 1)
                nc.scalar.activation(xT[:, :, :], xT_ps[:, :, :], ACT.Copy).then_inc(xT_ready, 1)

            def evacuate_gi(n, parity, g):
                act.wait_ge(gi_done[g], n + 1)
                for k in range(K):
                    last = nc.scalar.activation(giT[:, parity, g, k, :], gi_ps[g][:, k, :], ACT.Identity,
                                                bias=gate_bias[:, g, k:k + 1])
                last.then_inc(giT_ready[g], 1)

            def tanh_r(t, a):
                act.wait_ge(pre_r_ready[a], t + 1)
                nc.scalar.activation(th_r[:, HALF[a], :], pre_r[:, HALF[a], :], ACT.Tanh,
                                     scale=0.5).then_inc(th_r_ready[a], 1)

            def tanh_z(t, a):
                act.wait_ge(pre_z_ready[a], t + 1)
                nc.scalar.activation(th_z[:, HALF[a], :], pre_z[:, HALF[a], :], ACT.Tanh,
                                     scale=0.5).then_inc(th_z_ready[a], 1)

            def tanh_n(t, a):
                act.wait_ge(pre_n_ready[a], t + 1)
                nc.scalar.activation(n_t[:, HALF[a], :], pre_n[:, HALF[a], :], ACT.Tanh).then_inc(n_ready[a], 1)

            def turn(m, first, last):
                for par in range(2):
                    i = m * 2 + par
                    for s in range(TT):
                        t = m * BODY + (par * TT + s)
                        has_next = not (last and par == 1)
                        if s == 0 and not (first and par == 0):
                            evacuate_gi(i, par, 2)
                        if s == 1 and has_next:
                            evacuate_xT(i + 1)
                        if s == 5 and has_next:
                            evacuate_gi(i + 1, 1 - par, 0)
                        if s == 7 and has_next:
                            evacuate_gi(i + 1, 1 - par, 1)
                        tanh_r(t, 0)
                        tanh_z(t, 0)
                        tanh_n(t, 0)
                        tanh_r(t, 1)
                        tanh_z(t, 1)
                        tanh_n(t, 1)

            evacuate_xT(0)
            act.wait_ge(bias_ready, 1)
            for g in range(G):
                evacuate_gi(0, 0, g)
            turn(0, True, False)
            with act.Fori(1, TURNS - 1) as m:
                turn(m, False, False)
            turn(TURNS - 1, False, True)
            act.wait_ge(shifted, 1)
            nc.scalar.activation(scores, scores, ACT.Exp).then_inc(soft_exp, 1)
            with act.Fori(0, NT // 2) as m:
                act.wait_ge(out_ready, m * 2 + 2)
                act.dma_start(out_tiles[m * 2 + 1], ffn[:, m * 2 + 1, :]).then_inc(stored, 16)

        @block.tensor
        def _(pe):
            def transpose_x(n, parity, loads):
                pe.wait_ge(x_loaded[parity], loads)
                for kc in range(K):
                    mm = nc.tensor.transpose(xT_ps[:, kc, :], x_in[:, parity, kc * P:(kc + 1) * P], ident[:, :])
                mm.then_inc(xT_done, 1)

            def project(n, g, k, kc, prior):
                if g == 0 and k == 0 and kc == 0:
                    pe.wait_ge(xT_ready, n + 1)
                if k == 0 and kc == 0 and prior:
                    pe.wait_ge(giT_ready[g], n)
                first = g * D + k * P
                mm = nc.tensor.matmul(gi_ps[g][:, k, :], wih[:, kc, first:first + P], xT[:, kc, :], start=(kc == 0), stop=(kc == K - 1),
                                      skip_group_check=True)
                if k == K - 1 and kc == K - 1:
                    mm.then_inc(gi_done[g], 1)

            def expert(n, par, k, prior):
                if k == 0 and prior:
                    pe.wait_ge(ffn_stored, n)
                mm = nc.tensor.matmul(ffn_ps[:, :], hist[:, par, k, :], we[:, k, :], start=(k == 0), stop=(k == K - 1))
                if k == K - 1:
                    mm.then_inc(ffn_done, 1)

            def router(n, par, prior):
                if prior:
                    pe.wait_ge(log_stored, n)
                for k in range(K):
                    mm = nc.tensor.matmul(log_ps[:, :], hist[:, par, k, :], wr[:, k, :], start=(k == 0), stop=(k == K - 1))
                mm.then_inc(log_done, 1)

            def recurrent(t, par, s):
                hp, hs = (par, s - 1) if s else (1 - par, TT - 1)
                for k in range(K):
                    if k % (K // 2) == 0:
                        pe.wait_ge(h_ready[k // (K // 2)], t + 1)
                    for j in range(J):
                        mm = nc.tensor.matmul(
                            gh_ps[Q * j:Q * j + B, :, :].rearrange("b g (k c) -> b (g k) c", c=Q),
                            hist[:, hp, k, hs * B:(hs + 1) * B],
                            whh[:, k, :].rearrange("p (r j c) -> p j r c", j=J, c=Q)[:, j],
                            start=(k == 0), stop=(k == K - 1))
                mm.then_inc(gh_done, 1)

            GI = [(g, k, kc) for g in range(G) for k in range(K) for kc in range(K)]
            GI_STEPS = [0, 4, 4, 4, 9, 9, 9, 9]

            def turn(m, first, last):
                for par in range(2):
                    i = m * 2 + par
                    has_next = not (last and par == 1)
                    has_prior = not (first and par == 0)
                    at = 0
                    for s in range(TT):
                        recurrent(m * BODY + (par * TT + s), par, s)
                        if s == 0 and has_next:
                            transpose_x(i + 1, 1 - par, (m + par) * 16 + 16)
                        if s < K and has_prior:
                            expert(i - 1, 1 - par, s, not (first and par == 1))
                        if s == 0 and has_prior:
                            router(i - 1, 1 - par, not (first and par == 1))
                        if has_next:
                            for g, k, kc in GI[at:at + GI_STEPS[s]]:
                                project(i + 1, g, k, kc, True)
                            at += GI_STEPS[s]

            pe.wait_ge(masks_ready, 1)
            transpose_x(0, 0, 16)
            pe.wait_ge(w_early, (K + 2 * J) * 16)
            for g, k, kc in GI:
                project(0, g, k, kc, False)
            pe.wait_ge(w_late, (3 * J + 2) * 16)
            turn(0, True, False)
            with pe.Fori(1, TURNS - 1) as m:
                turn(m, False, False)
            turn(TURNS - 1, False, True)
            pe.wait_ge(h_ready[0], T + 1)
            pe.wait_ge(h_ready[1], T + 1)
            router(NT - 1, 1, True)
            for k in range(K):
                expert(NT - 1, 1, k, True)
            pe.wait_ge(scores_ready, 1)
            for g in range(NG):
                mm = nc.tensor.transpose(xT_ps[:, g, :],
                                         scores_g[:, g, :], ident[:, :])
            mm.then_inc(ST_done, 1)
            def sum_counts(r):
                pe.wait_ge(cnt_own, r + 1)
                nc.tensor.matmul(cnt_ps[:, 0:3], same_expert[:, :], cnt[:, :], start=True, stop=True).then_inc(cnt_all, 1)

            sum_counts(0)
            with pe.Fori(0, ROUNDS // 2) as r:
                sum_counts(r * 2 + 1)
                sum_counts(r * 2 + 2)
            sum_counts(ROUNDS)
            pe.wait_ge(R_ready, 1)
            nc.tensor.matmul(gi_ps[0][:, 0, 0:B], same_expert[:, :], R[:, :], start=True, stop=True)
            nc.tensor.matmul(gi_ps[1][:, 0, 0:B], before[:, :], R[:, :], start=True, stop=True).then_inc(R_summed, 1)
            pe.wait_ge(chosen_ready, 1)
            for g in range(NG):
                mm = nc.tensor.matmul(gi_ps[2][:, 0, g * NI:(g + 1) * NI],
                                      chosen[:, g * P:(g + 1) * P],
                                      group_of[:, :], start=True, stop=True, skip_group_check=True)
            mm.then_inc(weight_done, 1)

        @block.vector
        def _(dve):
            V = nc.vector
            V.memset(b_rows[:, :, :], 0.0)
            V.memset(h0[:, :], 0.0).then_inc(start_zeroed, 1)
            V.memset(gh_ps[:, :, :], 0.0)
            dve.wait_ge(w_early, (K + 2 * J) * 16)
            V.transpose(b_cols[:, :, :], b_rows[:, :, :]).then_inc(b_turned, 1)
            dve.wait_ge(b_turned, 1)
            bi, bh = (b_cols[:, n, 0:G * K].rearrange("p (g k) -> p g k", g=G) for n in range(2))
            V.tensor_tensor(gate_bias[:, 0:2, :], bi[:, 0:2, :], bh[:, 0:2, :], ALU.add)
            V.tensor_copy(gate_bias[:, 2, :], bi[:, 2, :]).then_inc(bias_ready, 1)
            dve.wait_ge(masks_ready, 1)
            for k in range(K):
                V.tensor_scalar(hn_bias[:, k, :], zeros[:, :], bh[:, 2, k:k + 1], 0.5, ALU.add, ALU.mult)
            dve.wait_ge(h0_loaded, J * 16)
            V.transpose(raw[:, 0, :], h0[:, :]).then_inc(h0_turned, 1)
            dve.wait_ge(h0_turned, 1)
            first_state = raw[:, 0, :].rearrange("p (k q) -> p k q", q=Q)[:, :, 0:B]
            V.tensor_scalar(half_h[:, :, :], first_state, 0.5, None, ALU.mult).then_inc(half_h_ready, 1)
            for a in range(2):
                V.tensor_copy(hist[:, 1, HALF[a], (TT - 1) * B:TT * B], first_state[:, HALF[a]]).then_inc(h_ready[a], 1)
            dve.wait_ge(w_late, (3 * J + 2) * 16)

            raw_k = raw[:, :, :].rearrange("p g (k q) -> p g k q", q=Q)

            def step(t, par, s):
                cols = slice(s * B, (s + 1) * B)

                def turned(gate, half, done):
                    V.transpose(raw[:, gate, half], gh_ps[:, gate, half]).then_inc(done, 1)

                def add_gi_r(a):
                    dve.wait_ge(raw_r[a], t + 1)
                    V.tensor_tensor(pre_r[:, HALF[a], :], raw_k[:, 0, HALF[a], 0:B], giT[:, par, 0, HALF[a], cols],
                                    ALU.add).then_inc(pre_r_ready[a], 1)

                def add_gi_z(a):
                    dve.wait_ge(raw_z[a], t + 1)
                    V.tensor_tensor(pre_z[:, HALF[a], :], raw_k[:, 1, HALF[a], 0:B], giT[:, par, 1, HALF[a], cols],
                                    ALU.add).then_inc(pre_z_ready[a], 1)

                def add_hn_bias(a):
                    V.scalar_tensor_tensor(hnb[:, HALF[a], :], raw_k[:, 2, HALF[a], 0:B], 0.5, hn_bias[:, HALF[a], :],
                                           ALU.mult, ALU.add).then_inc(hnb_ready[a], 1)

                def reset_hn(a):
                    V.scalar_tensor_tensor(rh[:, HALF[a], :], th_r[:, HALF[a], :], 1.0, hnb[:, HALF[a], :],
                                           ALU.add, ALU.mult).then_inc(rh_ready[a], 1)

                def add_gi_n(a):
                    dve.wait_ge(rh_ready[a], t + 1)
                    V.tensor_tensor(pre_n[:, HALF[a], :], rh[:, HALF[a], :], giT[:, par, 2, HALF[a], cols],
                                    ALU.add).then_inc(pre_n_ready[a], 1)

                def z_times_h(a):
                    dve.wait_ge(th_z_ready[a], t + 1)
                    V.scalar_tensor_tensor(zh[:, HALF[a], :], th_z[:, HALF[a], :], 1.0, half_h[:, HALF[a], :],
                                           ALU.add, ALU.mult)

                def n_part(a):
                    dve.wait_ge(n_ready[a], t + 1)
                    V.scalar_tensor_tensor(nz[:, HALF[a], :], th_z[:, HALF[a], :], 1.0, n_t[:, HALF[a], :],
                                           ALU.subtract, ALU.mult).then_inc(nz_ready[a], 1)

                def new_state(a):
                    dve.wait_ge(nz_ready[a], t + 1)
                    V.scalar_tensor_tensor(hist[:, par, HALF[a], cols], nz[:, HALF[a], :], -0.5, zh[:, HALF[a], :],
                                           ALU.mult, ALU.add).then_inc(h_ready[a], 1)

                half = (slice(0, P // 2), slice(P // 2, P))
                dve.wait_ge(gh_done, t + 1)
                turned(0, half[0], raw_r[0])
                turned(2, half[0], raw_n[0])
                add_gi_r(0)
                dve.wait_ge(raw_n[0], t + 1)
                add_hn_bias(0)
                turned(1, half[0], raw_z[0])
                dve.wait_ge(hnb_ready[0], t + 1)
                turned(0, half[1], raw_r[1])
                dve.wait_ge(th_r_ready[0], t + 1)
                reset_hn(0)
                add_gi_z(0)
                add_gi_n(0)
                add_gi_r(1)
                turned(2, half[1], raw_n[1])
                z_times_h(0)
                n_part(0)
                turned(1, half[1], raw_z[1])
                new_state(0)
                dve.wait_ge(th_r_ready[1], t + 1)
                add_hn_bias(1)
                add_gi_z(1)
                dve.wait_ge(hnb_ready[1], t + 1)
                reset_hn(1)
                add_gi_n(1)
                z_times_h(1)
                n_part(1)
                new_state(1)
                dve.wait_ge(h_ready[1], t + 2)
                V.tensor_scalar(half_h[:, :, :], hist[:, par, :, cols], 0.5, None, ALU.mult).then_inc(half_h_ready, 1)

            def store_logits(n):
                dve.wait_ge(log_done, n + 1)
                V.tensor_tensor(logits[:, n, :], log_ps[:, :], br[:, :], ALU.add).then_inc(log_stored, 1)

            def store_ffn(n, c):
                half = slice(c * D // 2, (c + 1) * D // 2)
                if c == 0:
                    dve.wait_ge(ffn_done, n + 1)
                ins = V.tensor_tensor(ffn[:, n, half], ffn_ps[:, half], be[:, half], ALU.add)
                if c == 1:
                    ins.then_inc(ffn_stored, 1)

            def turn(m, first, last):
                for par in range(2):
                    i = m * 2 + par
                    for g in range(G):
                        dve.wait_ge(giT_ready[g], i + 1)
                    for s in range(TT):
                        step(m * BODY + (par * TT + s), par, s)
                        if not (first and par == 0):
                            if s == 1:
                                store_logits(i - 1)
                            if s in (4, 5):
                                store_ffn(i - 1, s - 4)

            turn(0, True, False)
            with dve.Fori(1, TURNS - 1) as m:
                turn(m, False, False)
            turn(TURNS - 1, False, True)
            store_logits(NT - 1)

            chain = 0

            def link(ins):
                nonlocal chain
                chain += 1
                ins.then_inc(soft, 1)
                dve.wait_ge(soft, chain)

            dve.wait_ge(log_stored, NT)
            link(V.tensor_reduce(row[:, :], scores, AX.X, ALU.max))
            V.tensor_tensor(scores, scores, row[:, :].unsqueeze(2).broadcast_to([P, NT, NE]), ALU.subtract)\
                .then_inc(shifted, 1)
            V.memset(zeros_w, 0.0)
            V.memset(thr[:, :], 0)
            for c in range(3):
                V.memset(cand[:, c:c + 1], (c + 1) << TOP_BIT - 1)
                V.memset(steps[:, 0, c:c + 1], (c + 1) << TOP_BIT - 1)
            dve.wait_ge(soft_exp, 1)
            link(V.tensor_reduce(row[:, :], scores, AX.X, ALU.add))
            link(V.reciprocal(row_inv[:, :], row[:, :]))
            V.tensor_tensor(scores_g.rearrange("p g (i e) -> p i g e", i=NI),
                            scores.rearrange("p (i g) e -> p i g e", g=NG),
                            row_inv[:, :].rearrange("p (i g) -> p i g", g=NG).unsqueeze(3).broadcast_to([P, NI, NG, NE]),
                            ALU.mult)\
                .then_inc(scores_ready, 1)
            store_ffn(NT - 1, 0)
            store_ffn(NT - 1, 1)
            dve.wait_ge(ST_done, 1)
            link(V.tensor_copy(S.rearrange("p (b g t) -> p b g t", b=B, g=NG),
                               xT_ps[:, :, :].rearrange("p g (t b) -> p b g t", b=B)))

            def refine(r, new, old, first=False):
                if not first:
                    dve.wait_ge(cnt_all, r)
                    V.tensor_scalar(reached[:, :], cnt_ps[:, 0:3], float(CAP), None, ALU.is_ge, ALU.add,
                                    accum_out=n_reached[:, :]).then_inc(reached_ready, 1)
                    dve.wait_ge(reached_ready, r)
                    V.tensor_tensor(kept[:, :], n_reached[:, :], steps[:, old, 0:1], ALU.mult).then_inc(kept_ready, 1)
                    dve.wait_ge(kept_ready, r)
                    V.scalar_tensor_tensor(cand[:, :], steps[:, new, :], kept[:, :], thr[:, :].broadcast_to([P, 3]),
                                           ALU.bitwise_or, ALU.bitwise_or).then_inc(cand_ready, 1)
                    dve.wait_ge(cand_ready, r)
                for c in range(3):
                    last = V.tensor_scalar(junk[c], S, cand[:, c:c + 1].bitcast(F32), None, ALU.is_ge, ALU.add,
                                           accum_out=cnt[:, c:c + 1])
                last.then_inc(cnt_own, 1)
                if not first:
                    V.tensor_tensor(thr[:, :], thr[:, :], kept[:, :], ALU.bitwise_or)
                V.tensor_scalar(steps[:, 1 - new, :], steps[:, new, :], 2, None, ALU.logical_shift_right)

            refine(0, 0, 1, True)
            with dve.Fori(0, ROUNDS // 2) as r:
                refine(r * 2 + 1, 1, 0)
                refine(r * 2 + 2, 0, 1)
            dve.wait_ge(cnt_all, ROUNDS)
            link(V.tensor_scalar(reached[:, :], cnt_ps[:, 0:3], float(CAP), None, ALU.is_ge, ALU.add,
                                 accum_out=n_reached[:, :]))
            link(V.tensor_tensor(kept[:, :], n_reached[:, :], steps[:, 0, 0:1], ALU.mult))
            link(V.tensor_tensor(thr[:, :], thr[:, :], kept[:, :], ALU.bitwise_or))
            thr_f = thr[:, :].bitcast(F32)
            V.tensor_scalar(above, S, thr_f, None, ALU.is_gt, ALU.add, accum_out=cnt[:, 0:1]).then_inc(cnt_own, 1)
            link(V.tensor_scalar(tie, S, thr_f, None, ALU.is_equal))
            V.tensor_reduce(R[:, :], tie.rearrange("p (b n) -> p b n", b=B), AX.X, ALU.add).then_inc(R_ready, 1)
            link(V.tensor_tensor_scan(prefix, tie, zeros_w, 0.0, ALU.add, ALU.add))
            dve.wait_ge(cnt_all, ROUNDS + 1)
            V.tensor_scalar(need[:, :], cnt_ps[:, 0:1], -1.0, float(CAP), ALU.mult, ALU.add)
            dve.wait_ge(R_ready, 1)
            dve.wait_ge(R_summed, 1)
            link(V.tensor_tensor(others[:, :], gi_ps[0][:, 0, 0:B], R[:, :], ALU.subtract))
            link(V.tensor_tensor_scan(scan_b[:, :], others[:, :], zeros[:, :], 0.0, ALU.add, ALU.add))
            link(V.tensor_tensor(offset[:, :], scan_b[:, :], others[:, :], ALU.subtract))
            link(V.tensor_tensor(offset[:, :], gi_ps[1][:, 0, 0:B], offset[:, :], ALU.add))
            link(V.tensor_tensor(rank.rearrange("p (b n) -> p b n", b=B), prefix.rearrange("p (b n) -> p b n", b=B),
                                 offset[:, :].unsqueeze(2).broadcast_to([P, B, NG * TT]), ALU.add))
            link(V.scalar_tensor_tensor(rank, rank, need[:, :], tie, ALU.is_le, ALU.mult))
            link(V.tensor_tensor(above, above, rank, ALU.add))
            by_token = "p (b g t) -> p b g t"
            V.tensor_tensor(chosen.rearrange("p (g t b) -> p b g t", g=NG, b=B), S.rearrange(by_token, b=B, g=NG),
                            above.rearrange(by_token, b=B, g=NG), ALU.mult).then_inc(chosen_ready, 1)
            dve.wait_ge(weight_done, 1)
            link(V.tensor_copy(weight[:, :, :], gi_ps[2][:, 0, 0:NG * NI].rearrange("p (g i) -> p g i", g=NG)))
            dve.wait_ge(ffn_stored, NT)
            for ph in range(NT // PH):
                dve.wait_ge(xs_loaded[ph], TT * 16)
                for o in range(PH):
                    n = ph * PH + o
                    V.scalar_tensor_tensor(ffn[:, n, :], ffn[:, n, :], weight[:, n % NG, n // NG:n // NG + 1],
                                           xs[:, n % XS, :], ALU.mult, ALU.add).then_inc(out_ready, 1)


_INS = ["x", "cond_2048", "L0_cond_W_ih", "L0_cond_W_hh", "L0_cond_b_ih", "L0_cond_b_hh", "L0_ffn_router_w",
        "L0_ffn_router_b", "L0_ffn_expert_w", "L0_ffn_expert_b"]


def kernel(**inputs):
    import numpy as _np
    import concourse.bacc as _bacc
    from concourse import mybir as _mybir
    from concourse.bass_utils import run_bass_kernel_spmd as _run

    nc = _bacc.Bacc("TRN2", target_bir_lowering=False, num_devices=1)
    arrays, args = {}, []
    for name in _INS:
        a = _np.ascontiguousarray(inputs[name])
        arrays[f"in_{name}"] = a
        args.append(nc.dram_tensor(f"in_{name}", a.shape, _mybir.dt.from_np(a.dtype), kind="ExternalInput").ap())
    shape = inputs["x"].shape
    args.append(nc.dram_tensor("out", shape, _mybir.dt.from_np(_np.dtype("float32")), kind="ExternalOutput").ap())
    gru_expert_choice_kernel(nc, *args)
    r = _run(nc, [arrays], core_ids=[0])
    return r.results[0]["out"]
```

```python
import concourse.bass as bass
from concourse import mybir
from contextlib import ExitStack


def gru_expert_choice_kernel(nc, x, cond, w_ih, w_hh, b_ih, b_hh, router_w, router_b, expert_w, expert_b, out):
    F32, F16, U16 = mybir.dt.float32, mybir.dt.float16, mybir.dt.uint16
    ALU = mybir.AluOpType
    ACT = mybir.ActivationFunctionType
    AX = mybir.AxisListType

    B, T, D = x.shape
    NE = router_w.shape[1]
    P = 128
    Q = 32
    J = P // Q
    K = D // P
    G = 3
    TT = P // B
    NT = T // TT
    BODY = 2 * TT
    TURNS = T // BODY
    CAP = (B * T) // NE
    NG = 4
    NI = NT // NG
    UPPER_ROUNDS, LOWER_ROUNDS = 14 // 2, 16 // 2
    XS = 24
    PH = 8
    FFN_LOADS = (3 + NI) * 16
    HALF = (slice(0, K // 2), slice(K // 2, K))

    x_tiles = x.rearrange("b (i t) d -> i t b d", t=TT)
    x_phases = x.rearrange("b (h i t) d -> h t b i d", t=TT, i=PH)
    out_tiles = out.rearrange("b (i t) d -> i t b d", t=TT)

    ctx = ExitStack()
    with ctx:
        def sb(name, shape, dt=F32):
            return ctx.enter_context(nc.sbuf_tensor(name, shape, dt))

        def pb(name, shape):
            return ctx.enter_context(nc.psum_tensor(name, shape, F32))

        def sem(name):
            return ctx.enter_context(nc.semaphore(name))

        whh = sb("whh", [P, K, G * D])
        wih = sb("wih", [P, K, G * D])
        we = sb("we", [P, K, D])
        WIN = P - NE
        wr_wide = sb("wr_wide", [P, K, WIN + P])
        wr_window = sb("wr_window", [P, K, P])
        be = sb("be", [P, D])
        br = sb("br", [P, 1])
        b_rows = sb("b_rows", [P, 2, Q])
        b_cols = sb("b_cols", [P, 2, Q])
        gate_bias = sb("gate_bias", [P, G, K])
        hn_bias = sb("hn_bias", [P, K, B])
        zeros = sb("zeros", [P, B])
        warm = sb("warm", [P, 2])
        ident = sb("ident", [P, P])
        x_in = sb("x_in", [P, 2, D])
        xT = sb("xT", [P, K, P])
        giT = sb("giT", [P, 2, G, K, P])
        hist = sb("hist", [P, 2, K, P])
        raw = sb("raw", [P, G, P])
        pre_rz = sb("pre_rz", [P, 2, K, B])
        th_rz = sb("th_rz", [P, 2, K, B, 2])
        hn_pair = sb("hn_pair", [P, K, B, 2])
        pre_n = sb("pre_n", [P, K, B, 2])
        n_t = sb("n_t", [P, K, B, 2])
        z_pair = sb("z_pair", [P, K, B, 2])
        half_h = sb("half_h", [P, K, B])
        state = sb("state", [P, 2, K, B, 2])
        ffn = sb("ffn", [P, NT, D])
        h0 = ffn[:, NT - 1, 0:P]
        xs = sb("xs", [P, XS, D])
        xs_late = whh[:, :, :].rearrange("p k c -> p (k c)").rearrange("p (n d) -> p n d", d=D)
        free = [wih[:, c // 3, (c % 3) * D:(c % 3 + 1) * D] for c in range(3 * K)]
        S, chosen, above, tie, prefix, rank, zeros_w = (free[c] for c in range(7))
        upper, lower = (free[7].bitcast(U16)[:, c * D:(c + 1) * D] for c in range(2))
        junk = [free[9].bitcast(U16)[:, 0:D], free[10].bitcast(U16)[:, 0:D], free[11].bitcast(U16)[:, 0:D]]
        logits_T = free[8]
        scores = logits_T.rearrange("p (n e) -> p n e", e=NE)
        same_expert = sb("same_expert", [P, P], F16)
        before = sb("before", [P, P], F16)
        group_of = sb("group_of", [P, NI])
        row = sb("row", [P, NT])
        row_inv = sb("row_inv", [P, NT])
        thr_upper = sb("thr_upper", [P, 1])
        thr_lower = sb("thr_lower", [P, 1])
        thr = sb("thr", [P, 1])
        target = sb("target", [P, 3])
        cand = sb("cand", [P, 3])
        steps = sb("steps", [P, 2, 6])
        base = sb("base", [P, 3])
        thr_away = sb("thr_away", [P, 1])
        cnt = sb("cnt", [P, 3], F16)
        reached = sb("reached", [P, 3])
        n_reached = sb("n_reached", [P, 1])
        need = sb("need", [P, 1])
        R = sb("R", [P, B], F16)
        others = sb("others", [P, B])
        scan_b = sb("scan_b", [P, B])
        offset = sb("offset", [P, B])
        fit = sb("fit", [P, B])
        weight = sb("weight", [P, NG, NI])

        gh_ps = [pb(f"gh_ps{p}", [P, G, P]) for p in range(2)]
        xT_ps = pb("xT_ps", [P, K, P])
        gi_ps = [pb(f"gi_ps{g}", [P, K, P]) for g in range(G)]
        ffn_ps = pb("ffn_ps", [P, D])
        log_ps = pb("log_ps", [P, NG, P])
        cnt_ps = gi_ps[0][:, 1, :]

        wih_loaded = [sem(f"wih_loaded{kc}") for kc in range(K)]
        whh_loaded = [sem(f"whh_loaded{k}") for k in range(K)]
        b_loaded = sem("b_loaded")
        ffn_w_loaded = sem("ffn_w_loaded")
        start_zeroed = sem("start_zeroed")
        ident_ready = sem("ident_ready")
        h0_loaded = sem("h0_loaded")
        h0_turned = sem("h0_turned")
        ident_cleared = sem("ident_cleared")
        masks_cleared = sem("masks_cleared")
        masks_step = sem("masks_step")
        masks_ready = sem("masks_ready")
        b_turned = sem("b_turned")
        bias_ready = sem("bias_ready")
        x_loaded = [sem(f"x_loaded{p}") for p in range(2)]
        xT_done = sem("xT_done")
        xT_ready = sem("xT_ready")
        gi_done = [sem(f"gi_done{g}") for g in range(G)]
        giT_ready = [sem(f"giT_ready{g}") for g in range(G)]
        gh_done = sem("gh_done")
        h_ready = [sem(f"h_ready{a}") for a in range(2)]
        raw_rz = [sem(f"raw_rz{a}") for a in range(2)]
        raw_n = sem("raw_n0")
        pre_rz_ready = [sem(f"pre_rz_ready{a}") for a in range(2)]
        th_rz_ready = [sem(f"th_rz_ready{a}") for a in range(2)]
        hn_pair_ready = [sem(f"hn_pair_ready{a}") for a in range(2)]
        pre_n_ready = [sem(f"pre_n_ready{a}") for a in range(2)]
        n_ready = [sem(f"n_ready{a}") for a in range(2)]
        z_pair_ready = [sem(f"z_pair_ready{a}") for a in range(2)]
        half_h_ready = sem("half_h_ready")
        hist_ready = sem("hist_ready")
        ffn_done = sem("ffn_done")
        ffn_stored = sem("ffn_stored")
        window_ready = sem("window_ready")
        log_done = sem("log_done")
        soft = sem("soft")
        soft_exp = sem("soft_exp")
        shifted = sem("shifted")
        cand_ready = sem("cand_ready")
        cnt_own = sem("cnt_own")
        cnt_all = sem("cnt_all")
        thr_moved = sem("thr_moved")
        thr_turned = sem("thr_turned")
        key_ready = sem("key_ready")
        cnt_act = sem("cnt_act")
        reached_ready = sem("reached_ready")
        R_ready = sem("R_ready")
        R_summed = sem("R_summed")
        chosen_ready = sem("chosen_ready")
        weight_done = sem("weight_done")
        xs_loaded = [sem(f"xs_loaded{p}") for p in range(NT // PH)]
        out_ready = sem("out_ready")
        stored = sem("stored")

        ctx.enter_context(nc.allow_low_precision(reason="whole numbers of at most D, exact in float16"))
        block = ctx.enter_context(nc.Block())

        @block.sync
        def _(sp):
            def load_x(n, parity):
                sp.dma_start(x_in[:, parity, :], x_tiles[n]).then_inc(x_loaded[parity], 16)

            load_x(0, 0)
            for kc in range(K):
                sp.dma_start(wih[:, kc, :], w_ih[kc * P:(kc + 1) * P, :]).then_inc(wih_loaded[kc], 16)
            sp.wait_ge(start_zeroed, 1)
            for j in range(J):
                sp.dma_start(h0[Q * j:Q * j + B, :],
                             cond.rearrange("b (k j c) -> j b k c", j=J, c=Q)[j]).then_inc(h0_loaded, 16)
            for k in range(K):
                sp.dma_start(whh[:, k, :], w_hh[k * P:(k + 1) * P, :]).then_inc(whh_loaded[k], 16)
            load_x(1, 1)
            sp.wait_ge(start_zeroed, 2)
            sp.dma_start(wr_wide[:, :, WIN:WIN + NE],
                         router_w.rearrange("(k p) e -> p k e", p=P)).then_inc(ffn_w_loaded, 16)
            for i in range(NI):
                sp.dma_start(br[i * NE:(i + 1) * NE, :],
                             router_b.rearrange("(e o) -> e o", o=1)).then_inc(ffn_w_loaded, 16)
            sp.dma_start(we[:, :, :], expert_w.rearrange("(k p) d -> p k d", p=P)).then_inc(ffn_w_loaded, 16)
            sp.dma_start(be[:, :], expert_b.partition_broadcast(P)).then_inc(ffn_w_loaded, 16)
            with sp.Fori(0, NT // 2 - 1) as m:
                for parity in range(2):
                    sp.wait_ge(xT_done, m * 2 + parity + 1)
                    load_x(m * 2 + parity + 2, parity)
            for ph in range(NT // PH):
                late = ph * PH >= XS
                if late:
                    sp.wait_ge(gh_done, T)
                for tt in range(TT):
                    slots = xs_late[:, 0:PH] if late else xs[:, ph * PH:(ph + 1) * PH]
                    sp.dma_start(slots[tt * B:(tt + 1) * B],
                                 x_phases[ph, tt]).then_inc(xs_loaded[ph], 16)
            with sp.Fori(0, NT // 2) as m:
                sp.wait_ge(out_ready, m * 2 + 1)
                sp.dma_start(out_tiles[m * 2], ffn[:, m * 2, :]).then_inc(stored, 16)
            sp.wait_ge(stored, NT * 16)

        @block.gpsimd
        def _(pool):
            step = 0

            def affine_select(out_, pattern, op, fill_, base, mult):
                return nc.gpsimd.affine_select(out=out_, in_=out_, pattern=pattern, compare_op=op, fill=fill_,
                                               base=base, channel_multiplier=mult)

            def select(out_, pattern, op, fill_, base, mult):
                nonlocal step
                if step:
                    pool.wait_ge(masks_step, step)
                step += 1
                affine_select(out_, pattern, op, fill_, base, mult).then_inc(masks_step, 1)

            nc.gpsimd.memset(ident[:, :], 0.0).then_inc(ident_cleared, 1)
            pool.wait_ge(ident_cleared, 1)
            affine_select(ident[:, :], [[-1, P]], ALU.not_equal, 1.0, 0, 1).then_inc(ident_ready, 1)
            nc.gpsimd.memset(same_expert[:, :], 0.0).then_inc(masks_cleared, 1)
            nc.gpsimd.memset(group_of[:, :], 1.0).then_inc(masks_cleared, 1)
            pool.wait_ge(masks_cleared, 2)
            for i in range(NI):
                select(same_expert[:, :], [[0, NI], [-1, NE]], ALU.not_equal, 1.0, -NE * i, 1)
            select(group_of[:, :], [[-NE, NI]], ALU.is_ge, 0.0, 0, 1)
            select(group_of[:, :], [[NE, NI]], ALU.is_ge, 0.0, NE - 1, -1)
            pool.wait_ge(masks_step, step)
            nc.gpsimd.tensor_copy(before[:, :], same_expert[:, :]).then_inc(masks_step, 1)
            step += 1
            pool.wait_ge(masks_step, step)
            affine_select(before[:, :], [[1, P]], ALU.is_gt, 0.0, 0, -1).then_inc(masks_ready, 1)

        @block.scalar
        def _(act):
            act.wait_ge(start_zeroed, 1)
            for j in range(J):
                for n, b in enumerate((b_ih, b_hh)):
                    act.dma_start(b_rows[Q * j:Q * j + G * K, n, :],
                                  b.rearrange("(r j c) -> j r c", j=J, c=Q)[j]).then_inc(b_loaded, 16)
            nc.scalar.activation(warm[:, 1:2], warm[:, 0:1], ACT.Tanh)

            def evacuate_xT(n):
                act.wait_ge(xT_done, n + 1)
                nc.scalar.activation(xT[:, :, :], xT_ps[:, :, :], ACT.Copy).then_inc(xT_ready, 1)

            def evacuate_gi(n, parity, g):
                act.wait_ge(gi_done[g], n + 1)
                for k in range(K):
                    last = nc.scalar.activation(giT[:, parity, g, k, :], gi_ps[g][:, k, :], ACT.Identity,
                                                bias=gate_bias[:, g, k:k + 1])
                last.then_inc(giT_ready[g], 1)

            def tanh_rz(t, a):
                act.wait_ge(pre_rz_ready[a], t + 1)
                nc.scalar.activation(th_rz[:, :, HALF[a], :, 1], pre_rz[:, :, HALF[a], :], ACT.Tanh,
                                     scale=0.5).then_inc(th_rz_ready[a], 1)

            def tanh_n(t, a):
                act.wait_ge(pre_n_ready[a], t + 1)
                nc.scalar.activation(n_t[:, HALF[a], :, 1], pre_n[:, HALF[a], :, 1], ACT.Tanh).then_inc(n_ready[a], 1)

            def keep_state(t, s):
                act.wait_ge(h_ready[1], t + 2)
                nc.scalar.activation(hist[:, s // TT % 2, :, s % TT * B:(s % TT + 1) * B], state[:, s % 2, :, :, 1],
                                     ACT.Copy).then_inc(hist_ready, 1)

            def move_window(m, first):
                if not first:
                    act.wait_ge(log_done, m * 2)
                offset = WIN if first else WIN - m // 2 * NE
                nc.scalar.activation(wr_window[:, :, :], wr_wide[:, :, bass.ds(offset, P)],
                                     ACT.Copy).then_inc(window_ready, 1)

            def turn(m, first, last):
                for par in range(2):
                    i = m * 2 + par
                    for s in range(TT):
                        t = m * BODY + (par * TT + s)
                        has_next = not (last and par == 1)
                        if not (first and par == 0 and s == 0):
                            keep_state(m * BODY + (par * TT + s - 1), (par * TT + s - 1) % BODY)
                        if s == 0 and not (first and par == 0):
                            evacuate_gi(i, par, 2)
                        if s == 1 and has_next:
                            evacuate_xT(i + 1)
                        if s == 3 and par == 0:
                            if first:
                                act.wait_ge(ffn_w_loaded, FFN_LOADS)
                            move_window(m, first)
                        if s == 5 and has_next:
                            evacuate_gi(i + 1, 1 - par, 0)
                        if s == 7 and has_next:
                            evacuate_gi(i + 1, 1 - par, 1)
                        tanh_rz(t, 0)
                        tanh_n(t, 0)
                        tanh_rz(t, 1)
                        tanh_n(t, 1)

            act.wait_ge(bias_ready, 1)
            for g in range(G):
                evacuate_gi(0, 0, g)
            turn(0, True, False)
            with act.Fori(1, TURNS - 1) as m:
                turn(m, False, False)
            turn(TURNS - 1, False, True)
            keep_state(T - 1, BODY - 1)
            act.wait_ge(shifted, 1)
            nc.scalar.activation(scores, scores, ACT.Exp).then_inc(soft_exp, 1)

            def count_third(r, key):
                act.wait_ge(cand_ready, r)
                nc.scalar.activation(junk[2], key, ACT.Sign, bias=cand[:, 2:3],
                                     accum_out=cnt[:, 2:3]).then_inc(cnt_act, 1)

            act.wait_ge(key_ready, 1)
            with act.Fori(1, UPPER_ROUNDS + 1) as r:
                count_third(r, upper)
            act.wait_ge(key_ready, 2)
            with act.Fori(UPPER_ROUNDS + 1, UPPER_ROUNDS + LOWER_ROUNDS + 1) as r:
                count_third(r, lower)
            with act.Fori(0, NT // 2) as m:
                act.wait_ge(out_ready, m * 2 + 2)
                act.dma_start(out_tiles[m * 2 + 1], ffn[:, m * 2 + 1, :]).then_inc(stored, 16)

        @block.tensor
        def _(pe):
            def transpose_x(n, parity, loads, chunks=range(K)):
                if chunks[0] == 0:
                    pe.wait_ge(x_loaded[parity], loads)
                for kc in chunks:
                    mm = nc.tensor.transpose(xT_ps[:, kc, :], x_in[:, parity, kc * P:(kc + 1) * P], ident[:, :])
                if chunks[-1] == K - 1:
                    mm.then_inc(xT_done, 1)

            def project(n, g, k, kc, prior, by_chunk=False):
                if g == 0 and k == 0 and kc == 0:
                    pe.wait_ge(xT_ready, n + 1)
                if k == 0 and kc == 0 and prior:
                    pe.wait_ge(giT_ready[g], n)
                first = g * D + k * P
                mm = nc.tensor.matmul(gi_ps[g][:, k, :], wih[:, kc, first:first + P], xT[:, kc, :],
                                      start=(kc == 0 and (k == 0 or not by_chunk)), stop=(kc == K - 1),
                                      skip_group_check=True)
                if k == K - 1 and kc == K - 1:
                    mm.then_inc(gi_done[g], 1)

            def expert(n, par, k, prior):
                if k == 0:
                    pe.wait_ge(hist_ready, n * TT + TT)
                    if prior:
                        pe.wait_ge(ffn_stored, n)
                mm = nc.tensor.matmul(ffn_ps[:, :], hist[:, par, k, :], we[:, k, :], start=(k == 0), stop=(k == K - 1))
                if k == K - 1:
                    mm.then_inc(ffn_done, 1)

            def router(n, par):
                pe.wait_ge(hist_ready, n * TT + TT)
                if par == 0:
                    pe.wait_ge(window_ready, n // 2 + 1)
                for k in range(K):
                    mm = nc.tensor.matmul(log_ps[:, n % NG, :], wr_window[:, k, :], hist[:, par, k, :],
                                          start=False, stop=(k == K - 1), skip_group_check=True)
                mm.then_inc(log_done, 1)

            def start_logits():
                nc.tensor.matmul(log_ps[:, :, :], ident[:, :], br[:, :].broadcast_to([P, NG * P]),
                                 start=True, stop=False, skip_group_check=True)

            def recurrent(t, par, s, loading):
                for k in range(K):
                    if k % (K // 2) == 0:
                        pe.wait_ge(h_ready[k // (K // 2)], t + 1)
                    if loading:
                        pe.wait_ge(whh_loaded[k], 16)
                    for j in range(J):
                        mm = nc.tensor.matmul(
                            gh_ps[s % 2][Q * j:Q * j + B, :, :].rearrange("b g (k c) -> b (g k) c", c=Q),
                            state[:, 1 - s % 2, k, :, 1],
                            whh[:, k, :].rearrange("p (r j c) -> p j r c", j=J, c=Q)[:, j],
                            start=(k == 0), stop=(k == K - 1))
                mm.then_inc(gh_done, 1)

            GI = [(g, k, kc) for g in range(G) for k in range(K) for kc in range(K)]
            GI_STEPS = [0, 5, 5, 5, 9, 8, 8, 8]
            AHEAD = 3

            def turn(m, first, last):
                for par in range(2):
                    i = m * 2 + par
                    has_next = not (last and par == 1)
                    has_prior = not (first and par == 0)
                    at = 0
                    for s in range(TT):
                        recurrent(m * BODY + (par * TT + s), par, s, first and par == 0 and s == 0)
                        if s == 0 and has_next:
                            transpose_x(i + 1, 1 - par, (m + par) * 16 + 16,
                                        range(K) if first and par == 0 else range(AHEAD, K))
                        if first and par == 1 and s == 0:
                            pe.wait_ge(ffn_w_loaded, FFN_LOADS)
                            start_logits()
                        if s < K and has_prior:
                            expert(i - 1, 1 - par, s, not (first and par == 1))
                        if s == 0 and has_prior:
                            router(i - 1, 1 - par)
                        if has_next:
                            for g, k, kc in GI[at:at + GI_STEPS[s]]:
                                project(i + 1, g, k, kc, True)
                            at += GI_STEPS[s]
                        if s >= TT - AHEAD and not last:
                            transpose_x(i + 2, par, m * 16 + 32, range(s - (TT - AHEAD), s - (TT - AHEAD) + 1))

            pe.wait_ge(ident_ready, 1)
            transpose_x(0, 0, 16)
            for kc in range(K):
                pe.wait_ge(wih_loaded[kc], 16)
                for g in range(G):
                    for k in range(K):
                        project(0, g, k, kc, False, by_chunk=True)
            turn(0, True, False)
            with pe.Fori(1, TURNS - 1) as m:
                turn(m, False, False)
            turn(TURNS - 1, False, True)
            router(NT - 1, 1)
            for k in range(K):
                expert(NT - 1, 1, k, True)
            def sum_counts(own, third=None):
                if third is not None:
                    pe.wait_ge(cnt_act, third)
                pe.wait_ge(cnt_own, own)
                c = 1 if third is None else 3
                nc.tensor.matmul(cnt_ps[:, 0:c], same_expert[:, :], cnt[:, 0:c],
                                 start=True, stop=True).then_inc(cnt_all, 1)

            pe.wait_ge(masks_ready, 1)
            with pe.Fori(1, UPPER_ROUNDS + 1) as r:
                sum_counts(r, r)
            sum_counts(UPPER_ROUNDS + 1)
            with pe.Fori(UPPER_ROUNDS + 2, UPPER_ROUNDS + LOWER_ROUNDS + 2) as r:
                sum_counts(r, r - 1)
            sum_counts(UPPER_ROUNDS + LOWER_ROUNDS + 2)
            pe.wait_ge(R_ready, 1)
            nc.tensor.matmul(gi_ps[1][:, 0, 0:B], same_expert[:, :], R[:, :], start=True, stop=True)
            nc.tensor.matmul(gi_ps[2][:, 0, 0:B], before[:, :], R[:, :], start=True, stop=True).then_inc(R_summed, 1)
            for g in range(NG):
                pe.wait_ge(chosen_ready, g + 1)
                mm = nc.tensor.matmul(xT_ps[:, 0, g * NI:(g + 1) * NI],
                                      chosen[:, g * P:(g + 1) * P],
                                      group_of[:, :], start=True, stop=True, skip_group_check=True)
            mm.then_inc(weight_done, 1)

        @block.vector
        def _(dve):
            V = nc.vector
            V.memset(b_rows[:, :, :], 0.0)
            V.memset(warm[:, :], 0.0)
            V.memset(h0, 0.0).then_inc(start_zeroed, 1)
            V.memset(wr_wide[:, :, :], 0.0).then_inc(start_zeroed, 1)
            V.memset(zeros[:, :], 0.0)
            V.memset(th_rz[:, :, :, :, :], 0.0)
            V.memset(n_t[:, :, :, :], 0.0)
            for p in range(2):
                V.memset(gh_ps[p][:, :, :], 0.0)
            dve.wait_ge(xT_done, 1)
            V.tensor_copy(xT[:, :, :], xT_ps[:, :, :]).then_inc(xT_ready, 1)
            dve.wait_ge(b_loaded, 2 * J * 16)
            V.transpose(b_cols[:, :, :], b_rows[:, :, :]).then_inc(b_turned, 1)
            dve.wait_ge(b_turned, 1)
            bi, bh = (b_cols[:, n, 0:G * K].rearrange("p (g k) -> p g k", g=G) for n in range(2))
            V.tensor_tensor(gate_bias[:, 0:2, :], bi[:, 0:2, :], bh[:, 0:2, :], ALU.add)
            V.scalar_tensor_tensor(gate_bias[:, 2, :], bh[:, 2, :], 0.5, bi[:, 2, :], ALU.mult, ALU.add)\
                .then_inc(bias_ready, 1)
            for k in range(K):
                V.tensor_scalar(hn_bias[:, k, :], zeros[:, :], bh[:, 2, k:k + 1], 0.5, ALU.add, ALU.mult)
            dve.wait_ge(h0_loaded, J * 16)
            V.transpose(raw[:, 0, :], h0[:, :]).then_inc(h0_turned, 1)
            dve.wait_ge(h0_turned, 1)
            first_state = raw[:, 0, :].rearrange("p (k q) -> p k q", q=Q)[:, :, 0:B]
            V.tensor_scalar(half_h[:, :, :], first_state, 0.5, None, ALU.mult).then_inc(half_h_ready, 1)
            for a in range(2):
                V.tensor_copy(state[:, 1, HALF[a], :, 1], first_state[:, HALF[a]]).then_inc(h_ready[a], 1)

            raw_k = raw[:, :, :].rearrange("p g (k q) -> p g k q", q=Q)

            def step(t, par, s):
                cols = slice(s * B, (s + 1) * B)

                def turned(gates, half, done=None):
                    ins = V.transpose(raw[:, gates, half], gh_ps[s % 2][:, gates, half])
                    if done is not None:
                        ins.then_inc(done, 1)

                def add_gi_rz(a):
                    dve.wait_ge(raw_rz[a], t + 1)
                    V.tensor_tensor(pre_rz[:, :, HALF[a], :], raw_k[:, 0:2, HALF[a], 0:B], giT[:, par, 0:2, HALF[a], cols],
                                    ALU.add).then_inc(pre_rz_ready[a], 1)

                def half_hn(a):
                    V.scalar_tensor_tensor(hn_pair[:, HALF[a], :, 0], raw_k[:, 2, HALF[a], 0:B], 0.5,
                                           hn_bias[:, HALF[a], :], ALU.mult, ALU.add)

                def half_hn_and_gi(a):
                    V.scalar_tensor_tensor(hn_pair[:, HALF[a], :, 1], raw_k[:, 2, HALF[a], 0:B], 0.5,
                                           giT[:, par, 2, HALF[a], cols], ALU.mult, ALU.add).then_inc(hn_pair_ready[a], 1)

                def pairs(buf, a):
                    return buf[:, HALF[a]].rearrange("p k b two -> p (k b two)")

                def sum_n(a):
                    V.tensor_tensor_scan(pairs(pre_n, a), pairs(th_rz[:, 0], a), pairs(hn_pair, a), 0.0,
                                         ALU.mult, ALU.add).then_inc(pre_n_ready[a], 1)

                def z_parts(a):
                    V.tensor_scalar(z_pair[:, HALF[a], :, 0], th_rz[:, 1, HALF[a], :, 1], -0.5, 0.5, ALU.mult, ALU.add)
                    V.scalar_tensor_tensor(z_pair[:, HALF[a], :, 1], th_rz[:, 1, HALF[a], :, 1], 1.0,
                                           half_h[:, HALF[a], :], ALU.add, ALU.mult).then_inc(z_pair_ready[a], 1)

                def new_state(a):
                    dve.wait_ge(n_ready[a], t + 1)
                    V.tensor_tensor_scan(pairs(state[:, s % 2], a), pairs(n_t, a), pairs(z_pair, a), 0.0,
                                         ALU.mult, ALU.add).then_inc(h_ready[a], 1)

                half = (slice(0, P // 2), slice(P // 2, P))
                dve.wait_ge(gh_done, t + 1)
                turned(slice(0, 2), half[0], raw_rz[0])
                turned(slice(2, 3), half[0], raw_n)
                add_gi_rz(0)
                dve.wait_ge(raw_n, t + 1)
                half_hn(0)
                half_hn_and_gi(0)
                turned(slice(2, 3), half[1])
                dve.wait_ge(hn_pair_ready[0], t + 1)
                turned(slice(0, 1), half[1])
                dve.wait_ge(th_rz_ready[0], t + 1)
                sum_n(0)
                z_parts(0)
                turned(slice(1, 2), half[1], raw_rz[1])
                dve.wait_ge(z_pair_ready[0], t + 1)
                half_hn(1)
                new_state(0)
                add_gi_rz(1)
                half_hn_and_gi(1)
                dve.wait_ge(hn_pair_ready[1], t + 1)
                dve.wait_ge(th_rz_ready[1], t + 1)
                sum_n(1)
                z_parts(1)
                dve.wait_ge(z_pair_ready[1], t + 1)
                new_state(1)
                dve.wait_ge(h_ready[1], t + 2)
                V.tensor_scalar(half_h[:, :, :], state[:, s % 2, :, :, 1], 0.5, None, ALU.mult).then_inc(half_h_ready, 1)

            def store_ffn(n, c):
                half = slice(c * D // 2, (c + 1) * D // 2)
                if c == 0:
                    dve.wait_ge(ffn_done, n + 1)
                ins = V.tensor_tensor(ffn[:, n, half], ffn_ps[:, half], be[:, half], ALU.add)
                if c == 1:
                    ins.then_inc(ffn_stored, 1)

            def turn(m, first, last):
                for par in range(2):
                    i = m * 2 + par
                    for g in range(G):
                        dve.wait_ge(giT_ready[g], i + 1)
                    for s in range(TT):
                        step(m * BODY + (par * TT + s), par, s)
                        if not (first and par == 0):
                            if s == 4 and first:
                                dve.wait_ge(ffn_w_loaded, FFN_LOADS)
                            if s in (4, 5):
                                store_ffn(i - 1, s - 4)

            turn(0, True, False)
            with dve.Fori(1, TURNS - 1) as m:
                turn(m, False, False)
            turn(TURNS - 1, False, True)
            chain = 0

            def link(ins):
                nonlocal chain
                chain += 1
                ins.then_inc(soft, 1)
                dve.wait_ge(soft, chain)

            def start_search(thr_part, rounds):
                V.memset(thr_part[:, :], 0.0)
                for c in range(3):
                    unit = float(1 << 2 * rounds - 2)
                    V.memset(steps[:, 0, c:c + 1], (unit, 2 * unit, -3 * unit)[c])
                    V.memset(steps[:, 0, 3 + c:4 + c], (unit, unit, -unit)[c])
                    last = V.memset(cand[:, c:c + 1], (unit, 2 * unit, 0.5 - 3 * unit)[c])
                last.then_inc(cand_ready, 1)

            dve.wait_ge(log_done, NT)
            link(V.transpose(logits_T, log_ps[:, :, :]))
            link(V.tensor_reduce(row[:, :], scores, AX.X, ALU.max))
            V.tensor_tensor(scores, scores, row[:, :].unsqueeze(2).broadcast_to([P, NT, NE]), ALU.subtract)\
                .then_inc(shifted, 1)
            V.memset(zeros_w, 0.0)
            V.memset(target[:, 0:2], float(CAP))
            V.memset(target[:, 2:3], float(2 * CAP - B * T))
            start_search(thr_upper, UPPER_ROUNDS)
            dve.wait_ge(soft_exp, 1)
            link(V.tensor_reduce(row[:, :], scores, AX.X, ALU.add))
            link(V.reciprocal(row_inv[:, :], row[:, :]))
            link(V.tensor_tensor(scores, scores, row_inv[:, :].unsqueeze(2).broadcast_to([P, NT, NE]), ALU.mult))
            link(V.transpose(S, logits_T))

            S_halves = S.bitcast(U16).rearrange("p (n two) -> p n two", two=2)
            V.tensor_copy(upper, S_halves[:, :, 1]).then_inc(key_ready, 1)

            def count(key):
                for c in range(2):
                    last = V.tensor_scalar(junk[c], key, cand[:, c:c + 1], None, ALU.is_ge, ALU.add,
                                           accum_out=cnt[:, c:c + 1])
                last.then_inc(cnt_own, 1)

            def prepare(thr_part, new, moved):
                V.tensor_scalar(thr_away[:, :], thr_part[:, :], -1.0, 0.5, ALU.mult, ALU.add).then_inc(thr_turned, 1)
                V.tensor_scalar(steps[:, 1 - new, :], steps[:, new, :], 0.25, None, ALU.mult)
                V.scalar_tensor_tensor(base[:, 0:2], steps[:, new, 0:2], 0.25, thr_part[:, :].broadcast_to([P, 2]),
                                       ALU.mult, ALU.add)
                dve.wait_ge(thr_turned, moved + 1)
                V.scalar_tensor_tensor(base[:, 2:3], steps[:, new, 2:3], 0.25, thr_away[:, :], ALU.mult, ALU.add)

            def reach(r, moved):
                dve.wait_ge(cnt_all, r)
                V.scalar_tensor_tensor(reached[:, :], cnt_ps[:, 0:3], 1.0, target[:, :], ALU.mult, ALU.is_ge,
                                       accum_out=n_reached[:, :]).then_inc(reached_ready, 1)
                dve.wait_ge(reached_ready, moved + 1)

            def move(out_, thr_part, last_steps):
                V.scalar_tensor_tensor(out_, steps[:, last_steps, 3:4], n_reached[:, :], thr_part[:, :],
                                       ALU.mult, ALU.add).then_inc(thr_moved, 1)

            def refine(r, moved, thr_part, key, new, turned):
                reach(r, moved)
                V.scalar_tensor_tensor(cand[:, :], steps[:, 1 - new, 3:6], n_reached[:, :],
                                       base[:, :], ALU.mult, ALU.add).then_inc(cand_ready, 1)
                move(thr_part[:, :], thr_part, 1 - new)
                dve.wait_ge(cand_ready, moved + 2)
                count(key)
                dve.wait_ge(thr_moved, moved + 1)
                prepare(thr_part, new, turned)

            dve.wait_ge(key_ready, 1)
            count(upper)
            prepare(thr_upper, 0, 0)
            store_ffn(NT - 1, 0)
            store_ffn(NT - 1, 1)
            with dve.Fori(0, (UPPER_ROUNDS - 1) // 2) as q:
                refine(q * 2 + 1, q * 2, thr_upper, upper, 1, q * 2 + 1)
                refine(q * 2 + 2, q * 2 + 1, thr_upper, upper, 0, q * 2 + 2)
            reach(UPPER_ROUNDS, UPPER_ROUNDS - 1)
            move(thr_upper[:, :], thr_upper, 0)
            dve.wait_ge(thr_moved, UPPER_ROUNDS)
            V.tensor_scalar(junk[0], upper, thr_upper[:, :], None, ALU.is_gt, ALU.add,
                            accum_out=cnt[:, 0:1]).then_inc(cnt_own, 1)
            V.tensor_copy(thr[:, :].bitcast(U16)[:, 1:2], thr_upper[:, :])
            start_search(thr_lower, LOWER_ROUNDS)
            V.scalar_tensor_tensor(lower, upper, thr_upper[:, :], S_halves[:, :, 0], ALU.is_equal, ALU.mult)\
                .then_inc(key_ready, 1)
            dve.wait_ge(cnt_all, UPPER_ROUNDS + 1)
            V.tensor_scalar(target[:, 0:2], cnt_ps[:, 0:1].broadcast_to([P, 2]), -1.0, float(CAP), ALU.mult, ALU.add)
            V.tensor_scalar(target[:, 2:3], cnt_ps[:, 0:1], -2.0, float(2 * CAP - B * T), ALU.mult, ALU.add)
            dve.wait_ge(key_ready, 2)
            count(lower)
            prepare(thr_lower, 0, UPPER_ROUNDS)
            LOW = UPPER_ROUNDS + 2
            with dve.Fori(0, (LOWER_ROUNDS - 1) // 2) as q:
                refine(q * 2 + LOW, q * 2 + UPPER_ROUNDS, thr_lower, lower, 1, q * 2 + UPPER_ROUNDS + 1)
                refine(q * 2 + LOW + 1, q * 2 + UPPER_ROUNDS + 1, thr_lower, lower, 0, q * 2 + UPPER_ROUNDS + 2)
            ALL_ROUNDS = UPPER_ROUNDS + LOWER_ROUNDS
            refine(ALL_ROUNDS, ALL_ROUNDS - 2, thr_lower, lower, 1, ALL_ROUNDS - 1)
            reach(ALL_ROUNDS + 1, ALL_ROUNDS - 1)
            move(thr[:, :].bitcast(U16)[:, 0:1], thr_lower, 1)
            dve.wait_ge(thr_moved, ALL_ROUNDS)
            dve.wait_ge(ffn_stored, NT)
            by_token = "p (b g t) -> p b g t"
            S_by_token = S.rearrange("p (g t b) -> p b g t", g=NG, b=B)
            def mark(ins):
                nonlocal chain
                chain += 1
                ins.then_inc(soft, 1)
                return chain

            V.tensor_scalar(above, S, thr[:, :], None, ALU.is_gt, ALU.add, accum_out=cnt[:, 0:1]).then_inc(cnt_own, 1)
            link(V.tensor_scalar(tie.rearrange(by_token, b=B, g=NG), S_by_token, thr[:, :], None, ALU.is_equal))
            V.tensor_reduce(R[:, :], tie.rearrange("p (b n) -> p b n", b=B), AX.X, ALU.add).then_inc(R_ready, 1)
            prefix_set = mark(V.tensor_tensor_scan(prefix, tie, zeros_w, 0.0, ALU.add, ALU.add))
            dve.wait_ge(cnt_all, ALL_ROUNDS + 2)
            V.tensor_scalar(need[:, :], cnt_ps[:, 0:1], -1.0, float(CAP), ALU.mult, ALU.add)
            dve.wait_ge(R_ready, 1)
            dve.wait_ge(R_summed, 1)
            others_set = mark(V.tensor_tensor(others[:, :], gi_ps[1][:, 0, 0:B], R[:, :], ALU.subtract))
            dve.wait_ge(soft, prefix_set)
            mark(V.tensor_tensor(rank, prefix, tie, ALU.mult))
            dve.wait_ge(soft, others_set)
            scan_set = mark(V.tensor_tensor_scan(scan_b[:, :], others[:, :], zeros[:, :], 0.0, ALU.add, ALU.add))
            mark(V.scalar_tensor_tensor(above, S, thr[:, :], S, ALU.is_ge, ALU.mult))
            dve.wait_ge(soft, scan_set)
            link(V.tensor_tensor(offset[:, :], scan_b[:, :], others[:, :], ALU.subtract))
            link(V.scalar_tensor_tensor(offset[:, :], offset[:, :], need[:, :], gi_ps[2][:, 0, 0:B],
                                        ALU.subtract, ALU.add))
            link(V.tensor_scalar(fit[:, :], offset[:, :], -1.0, 0.0, ALU.mult, ALU.max))
            link(V.tensor_tensor(prefix.rearrange("p (b n) -> p b n", b=B), rank.rearrange("p (b n) -> p b n", b=B),
                                 fit[:, :].unsqueeze(2).broadcast_to([P, B, NG * TT]), ALU.is_le))
            fits = prefix.rearrange("p (b g t) -> p g t b", b=B, g=NG)
            for g in range(NG):
                cols = slice(g * P, (g + 1) * P)
                V.tensor_tensor(chosen[:, cols].rearrange("p (t b) -> p t b", b=B),
                                above[:, cols].rearrange("p (t b) -> p t b", b=B), fits[:, g],
                                ALU.mult).then_inc(chosen_ready, 1)
            dve.wait_ge(weight_done, 1)
            link(V.tensor_copy(weight[:, :, :], xT_ps[:, 0, 0:NG * NI].rearrange("p (g i) -> p g i", g=NG)))
            for ph in range(NT // PH):
                dve.wait_ge(xs_loaded[ph], TT * 16)
                for o in range(PH):
                    n = ph * PH + o
                    V.scalar_tensor_tensor(ffn[:, n, :], ffn[:, n, :], weight[:, n % NG, n // NG:n // NG + 1],
                                           xs[:, n, :] if n < XS else xs_late[:, n - XS, :],
                                           ALU.mult, ALU.add).then_inc(out_ready, 1)


_INS = ["x", "cond_2048", "L0_cond_W_ih", "L0_cond_W_hh", "L0_cond_b_ih", "L0_cond_b_hh", "L0_ffn_router_w",
        "L0_ffn_router_b", "L0_ffn_expert_w", "L0_ffn_expert_b"]


def kernel(**inputs):
    import numpy as _np
    import concourse.bacc as _bacc
    from concourse import mybir as _mybir
    from concourse.bass_utils import run_bass_kernel_spmd as _run

    nc = _bacc.Bacc("TRN2", target_bir_lowering=False, num_devices=1)
    arrays, args = {}, []
    for name in _INS:
        a = _np.ascontiguousarray(inputs[name])
        arrays[f"in_{name}"] = a
        args.append(nc.dram_tensor(f"in_{name}", a.shape, _mybir.dt.from_np(a.dtype), kind="ExternalInput").ap())
    shape = inputs["x"].shape
    args.append(nc.dram_tensor("out", shape, _mybir.dt.from_np(_np.dtype("float32")), kind="ExternalOutput").ap())
    gru_expert_choice_kernel(nc, *args)
    r = _run(nc, [arrays], core_ids=[0])
    return r.results[0]["out"]
```
